# Optimizing a Trainium2 kernel written in Bass

```python
import numpy as np
import jax
import jax.numpy as jnp

def _softmax(x, axis=-1):
    return jax.nn.softmax(x, axis=axis)

def _gelu(x):
    return jax.nn.gelu(x, approximate=True)

def _silu(x):
    return jax.nn.silu(x)

def _sigmoid(x):
    return jax.nn.sigmoid(x)

def _layernorm(x, axis=-1, eps=1e-05):
    m = jnp.mean(x, axis=axis, keepdims=True)
    v = jnp.var(x, axis=axis, keepdims=True)
    return (x - m) / jnp.sqrt(v + eps)

def _scatter_add(tgt, idx, src, axis=0):
    return tgt.at[idx].add(src)

def _segment_sum(src, seg, n):
    return jax.ops.segment_sum(src, seg, n)
kernel_name = 'mk_flamingo_gated_d1_seqx_r4_1dce68'

def setup_inputs(seed: int=0):
    np.random.seed(seed)
    _w = jnp.asarray

    def _rec_inputs():
        import jax
        import jax.numpy as jnp
        _rk = jax.random.key(seed)
        x = -1.394e-06 + 0.9999 * jax.random.normal(jax.random.fold_in(_rk, 1), (16, 256, 256), jnp.float32)
        _lenS = 256 - jax.random.randint(jax.random.fold_in(_rk, 7), (16,), 0, max(1, 256 // 4) + 1, jnp.int32)
        _lenS2 = 256 - jax.random.randint(jax.random.fold_in(_rk, 8), (16,), 0, max(1, 256 // 4) + 1, jnp.int32)
        _ctx_1024P = jax.random.normal(jax.random.fold_in(_rk, 11), (16, 16, 256), jnp.float32)
        _ctx_1024c = jax.random.dirichlet(jax.random.fold_in(_rk, 511), 0.3 * jnp.ones((16,), jnp.float32), (16, 256))
        _ctx_1024t = jnp.einsum('bsk,bkd->bsd', _ctx_1024c, _ctx_1024P)
        _ctx_1024t = _ctx_1024t * jax.lax.rsqrt(jnp.mean(jnp.square(_ctx_1024t)) + 1e-12) * 0.953939
        ctx_1024 = -0.000292821 + 1.00034 * (_ctx_1024t + 0.3 * jax.random.normal(jax.random.fold_in(_rk, 611), (16, 256, 256), jnp.float32))
        _g = jax.random.normal(jax.random.fold_in(_rk, 9001), (2, 1), jnp.float32)
        _g = jnp.sign(_g) * jnp.maximum(jnp.abs(_g), 1.0) + (_g == 0) * 1.0
        g_xattn = _g[0]
        g_ffn = _g[1]
        return (x, ctx_1024, g_xattn, g_ffn)
    x, ctx_1024, g_xattn, g_ffn = _rec_inputs()

    def _L0_xattn_setup():
        import jax, jax.numpy as jnp
        import numpy as np
        NEG_INF = -1e+30
        key = jax.random.key(seed)
        ks = jax.random.split(key, 7)
        B, S, D, H, HD = (2, 512, 256, 16, 64)
        scale = 1.0 / np.sqrt(D)
        return {'keys': jax.random.normal(ks[0], (B, S, D), dtype=jnp.float32), 'queries': jax.random.normal(ks[1], (B, S, D), dtype=jnp.float32), 'values': jax.random.normal(ks[2], (B, S, D), dtype=jnp.float32), 'Wq': jax.random.normal(ks[3], (H, D, HD), dtype=jnp.float32) * scale, 'Wk': jax.random.normal(ks[4], (H, D, HD), dtype=jnp.float32) * scale, 'Wv': jax.random.normal(ks[5], (H, D, HD), dtype=jnp.float32) * scale, 'Wo': jax.random.normal(ks[6], (H * HD, D), dtype=jnp.float32) * scale}
    _L0_xattn_all = _L0_xattn_setup()
    _L0_xattn_in = {k: v for k, v in _L0_xattn_all.items() if k in ('Wq', 'Wk', 'Wv', 'Wo')}
    del _L0_xattn_all

    def _L0_ffn_setup():
        import math
        import jax, jax.numpy as jnp
        import numpy as np
        B, T, D = (4, 1024, 256)
        H = 16
        HD = D // H
        CAP = int(1024 * 0.125)
        DFF = int(D * 4 * 2 / 3)
        EPS = 1e-06

        def rmsnorm(x, g):
            return x * jax.lax.rsqrt(jnp.mean(x * x, axis=-1, keepdims=True) + EPS) * g
        key = jax.random.key(seed)
        ks = jax.random.split(key, 9)
        s = lambda k, shape: jax.random.normal(k, shape, jnp.float32) * 0.02
        return {'x': jax.random.normal(ks[0], (B, T, D), jnp.float32), 'w_router': s(ks[1], (D,)), 'W_qkv': s(ks[2], (3 * D, D)), 'W_out': s(ks[3], (D, D)), 'g1': jnp.ones((D,), jnp.float32), 'g2': jnp.ones((D,), jnp.float32), 'W1': s(ks[4], (DFF, D)), 'W2': s(ks[5], (DFF, D)), 'W3': s(ks[6], (D, DFF))}
    _L0_ffn_all = _L0_ffn_setup()
    _L0_ffn_in = {k: v for k, v in _L0_ffn_all.items() if k in ('w_router', 'W_qkv', 'W_out', 'g1', 'g2', 'W1', 'W2', 'W3')}
    del _L0_ffn_all
    return {'x': x, 'ctx_1024': ctx_1024, 'g_xattn': g_xattn, 'g_ffn': g_ffn, 'L0_xattn_Wq': _L0_xattn_in['Wq'], 'L0_xattn_Wk': _L0_xattn_in['Wk'], 'L0_xattn_Wv': _L0_xattn_in['Wv'], 'L0_xattn_Wo': _L0_xattn_in['Wo'], 'L0_ffn_w_router': _L0_ffn_in['w_router'], 'L0_ffn_W_qkv': _L0_ffn_in['W_qkv'], 'L0_ffn_W_out': _L0_ffn_in['W_out'], 'L0_ffn_g1': _L0_ffn_in['g1'], 'L0_ffn_g2': _L0_ffn_in['g2'], 'L0_ffn_W1': _L0_ffn_in['W1'], 'L0_ffn_W2': _L0_ffn_in['W2'], 'L0_ffn_W3': _L0_ffn_in['W3']}

def reference(x, ctx_1024, g_xattn, g_ffn, L0_xattn_Wq, L0_xattn_Wk, L0_xattn_Wv, L0_xattn_Wo, L0_ffn_w_router, L0_ffn_W_qkv, L0_ffn_W_out, L0_ffn_g1, L0_ffn_g2, L0_ffn_W1, L0_ffn_W2, L0_ffn_W3):
    import jax
    import jax.numpy as jnp

    def _L0_xattn_ref(keys, queries, values, Wq, Wk, Wv, Wo):
        import jax, jax.numpy as jnp
        import numpy as np
        NEG_INF = -1e+30
        B, S, D = keys.shape
        H, _, HD = Wq.shape
        q = jnp.einsum('bsd,hde->bhse', queries, Wq)
        k = jnp.einsum('bsd,hde->bhse', keys, Wk)
        v = jnp.einsum('bsd,hde->bhse', values, Wv)
        scores = jnp.einsum('bhqe,bhke->bhqk', q, k) / jnp.sqrt(jnp.float32(HD))
        tril = jnp.tril(jnp.ones((S, S), dtype=bool))
        scores = jnp.where(tril, scores, NEG_INF)
        attn = jax.nn.softmax(scores, axis=-1)
        out = jnp.einsum('bhqk,bhke->bhqe', attn, v)
        concat = out.transpose(0, 2, 1, 3).reshape(B, S, H * HD)
        return concat @ Wo

    def _L0_ffn_ref(x, w_router, W_qkv, W_out, g1, g2, W1, W2, W3):
        import math
        import jax, jax.numpy as jnp
        import numpy as np
        B, T, D = (4, 1024, 256)
        H = 16
        HD = D // H
        CAP = int(1024 * 0.125)
        DFF = int(D * 4 * 2 / 3)
        EPS = 1e-06

        def rmsnorm(x, g):
            return x * jax.lax.rsqrt(jnp.mean(x * x, axis=-1, keepdims=True) + EPS) * g
        Bq, Tq, Dq = x.shape
        scores = x @ w_router
        _, idx = jax.lax.top_k(scores, CAP)
        x_sel = jnp.take_along_axis(x, idx[:, :, None], axis=1)
        h = rmsnorm(x_sel, g1)
        qkv = (h @ W_qkv.T).reshape(Bq, CAP, 3, H, HD)
        q, k, v = jnp.moveaxis(qkv, 2, 0)
        att = jnp.einsum('bqhd,bkhd->bhqk', q, k) / math.sqrt(HD)
        mask = jnp.triu(jnp.ones((CAP, CAP), bool), 1)
        att = jnp.where(mask, -jnp.inf, att)
        att = jax.nn.softmax(att, axis=-1)
        o = jnp.einsum('bhqk,bkhd->bqhd', att, v).reshape(Bq, CAP, Dq)
        x_attn = o @ W_out.T
        h2 = rmsnorm(x_sel + x_attn, g2)
        x_ff = jax.nn.silu(h2 @ W1.T) * (h2 @ W2.T) @ W3.T
        x_proc = x_sel + x_attn + x_ff
        out = x.at[jnp.arange(Bq)[:, None], idx].set(x_proc)
        return out
    x = x + jnp.tanh(g_xattn[0]) * _L0_xattn_ref(ctx_1024, _layernorm(x, axis=-1), ctx_1024, L0_xattn_Wq, L0_xattn_Wk, L0_xattn_Wv, L0_xattn_Wo)
    x = x + jnp.tanh(g_ffn[0]) * _L0_ffn_ref(_layernorm(x, axis=-1), L0_ffn_w_router, L0_ffn_W_qkv, L0_ffn_W_out, L0_ffn_g1, L0_ffn_g2, L0_ffn_W1, L0_ffn_W2, L0_ffn_W3)
    return x

_drawn_inputs = setup_inputs


def setup_inputs(seed=0):
    import zlib

    import numpy as np

    out = dict(_drawn_inputs(seed))
    spreads = {'L0_ffn_g1': (1.0, 0.6), 'L0_ffn_g2': (1.0, 0.6)}
    factors = {}
    for name, (base, spread) in spreads.items():
        noise = np.random.default_rng([zlib.crc32(name.encode()), seed]).standard_normal(out[name].shape)
        drawn = base * np.exp(spread * noise) if base else spread * noise
        out[name] = jnp.asarray(drawn.astype(out[name].dtype))
    for name, factor in factors.items():
        out[name] = (out[name] * factor).astype(out[name].dtype)
    return out
```

```python
from contextlib import ExitStack

import concourse.bass as bass
from concourse import mybir

ALU = mybir.AluOpType
ACT = mybir.ActivationFunctionType
F32 = mybir.dt.float32
F32R = mybir.dt.float32r
BF16 = mybir.dt.bfloat16

P = 128
B, S, D = 16, 256, 256
H, HD = 16, 64
NT = S // P
NC = D // P
HP = H // 2
CAP = 128
FH, FHD = 16, 16
DFF = D * 4 * 2 // 3
NF = (DFF + P - 1) // P
FR = DFF - (NF - 1) * P
FCH = [(0, 342), (342, DFF - 342)]
BIG = 1e30


def need(eng, sem, per, b, c):
    v = b * per + c
    if isinstance(v, int) and v <= 0:
        return
    eng.wait_ge(sem, v)


def need_apart(eng, sem, per, b, c, passed):
    need(eng, sem, per, b, c)
    if not isinstance(b, int):
        eng.sem_inc(passed, 1)


def f32(ap):
    return ap.bitcast(F32)


def build(nc, x, ctx_in, g_xattn, g_ffn, Wq, Wk, Wv, Wo, w_router, W_qkv, W_out, g1, g2, W1, W2, W3, out):
    with ExitStack() as es:
        def sb(name, shape, dt=F32):
            return es.enter_context(nc.sbuf_tensor(name, shape, dt))

        def sem(name):
            return es.enter_context(nc.semaphore(name))

        bkQ = es.enter_context(nc.psum_tensor("bkQ", [P, 512], F32))
        bkK = es.enter_context(nc.psum_tensor("bkK", [P, 512], F32))
        bkS1 = es.enter_context(nc.psum_tensor("bkS1", [P, 512], F32))
        bkS0 = es.enter_context(nc.psum_tensor("bkS0", [P, 512], F32))
        bkP = es.enter_context(nc.psum_tensor("bkP", [P, 512], F32))
        bkO = es.enter_context(nc.psum_tensor("bkO", [P, 512], F32))
        bkA = es.enter_context(nc.psum_tensor("bkA", [P, 512], F32))
        bkB = es.enter_context(nc.psum_tensor("bkB", [P, 512], F32))

        ident = sb("ident", [P, P])
        mask = sb("mask", [P, 2 * P], BF16)
        tri = sb("tri", [P, NT, S], BF16)
        iota = sb("iota", [P, P])
        wrow = sb("wrow", [P, D])
        mhalf = sb("mhalf", [P, NT])
        gcol = sb("gcol", [P, 2])
        tg = sb("tg", [P, 2])
        g1c = sb("g1c", [P, NC])
        g2c = sb("g2c", [P, NC])

        wqX = sb("wqX", [P, 2, NC, H * HD], F32R)
        wkX = sb("wkX", [P, 2, NC, H * HD], F32R)
        wvX = sb("wvX", [P, 2, NC, H * HD], F32R)
        woX = sb("woX", [P, 2, HP, D], F32R)
        wqkvX = sb("wqkvX", [P, 2, NC, 3 * D], F32R)
        woutX = sb("woutX", [P, 2, NC, D], F32R)
        w1X = sb("w1X", [P, 2, NC, DFF], F32R)
        w2X = sb("w2X", [P, 2, NC, DFF], F32R)
        w3X = sb("w3X", [P, 2, NF, D], F32R)

        xin = sb("xin", [P, NT, D])
        cin = sb("cin", [P, NT, D])
        zX = sb("zX", [P, 2, NC, S], F32R)
        cX = sb("cX", [P, 2, NC, S], F32R)
        vX = sb("vX", [P, 2, 2, NT, 512], F32R)
        qX = sb("qX", [P, 2, S], F32R)
        kX = sb("kX", [P, 2, 2, S], F32R)
        pm = sb("pm", [P, 2, 768])
        p0X = sb("p0X", [P, 2, 2, S], F32R)
        p1X = sb("p1X", [P, 2, 2, P], F32R)
        oX = sb("oX", [P, 2, HP // 2, S], F32R)
        bst = sb("bst", [P, NT, 6])
        mv = sb("mv", [P, NT, 2])
        ve = sb("ve", [P, NT])
        rs = sb("rs", [P, NT])
        rsn = sb("rsn", [P, NT])
        mn = sb("mn", [P, 2, 4])
        sm = sb("sm", [P, 2, 4])
        ri = sb("ri", [P, 2, 4])

        x1 = sb("x1", [P, NT, D])
        stage1 = sb("stage1", [P, 2048])
        y = stage1[:, 0:512].rearrange("p (t d) -> p t d", t=NT)
        xs = stage1[:, 512:768]
        u = stage1[:, 768:1024]
        ot = stage1[:, 1024:1536].rearrange("p (t d) -> p t d", t=NT)
        pfx = stage1[:, 1536:2048]
        h = sb("h", [P, D])
        bst2 = sb("bst2", [P, NT, 6])
        mv2 = sb("mv2", [P, NT, 2])
        ve2 = sb("ve2", [P, NT])
        rs2 = sb("rs2", [P, NT])
        sc = sb("sc", [P, NT])
        junk = stage1[:, 512:1024].bitcast(BF16).rearrange("p (j n) -> p j n", j=4)
        ra = sb("ra", [P, NT])
        rb = sb("rb", [P, NT])
        rank = sb("rank", [P, NT])
        nst = sb("nst", [P, NT])
        ms = sb("ms", [P, 2])
        rr = sb("rr", [P, 2])
        perm = sb("perm", [P, NT, P], F32R)
        permT = sb("permT", [P, S], F32R)
        hX = sb("hX", [P, 2, NC, P], F32R)
        r1X = sb("r1X", [P, 1536], F32R)
        r2X = sb("r2X", [P, 1536], F32R)
        vf = sb("vf", [P, D])
        stage0 = sb("stage0", [P, 2048])
        sf = stage0[:, 0:1024].rearrange("p (r t k) -> p r t k", r=2, t=4)
        pf = stage0[:, 1024:2048].rearrange("p (r t k) -> p r t k", r=2, t=4)
        gb = stage0[:, 0:DFF]
        eb = stage0[:, 1024:1024 + 342]
        mf = sb("mf", [P, FH])
        sumf = sb("sumf", [P, FH])
        rif = sb("rif", [P, FH])
        yX = r2X[:, 0:1024].rearrange("p (s t d) -> p s t d", s=2, t=NT)
        qkp = r2X[:, :].rearrange("p (a h e) -> p a h e", a=3, h=FH)
        xpX = r2X[:, 0:512].rearrange("p (s d) -> p s d", s=2)
        qkT = r1X[:, :].rearrange("p (a t n) -> p a t n", a=3, t=4)
        gX = r1X[:, :].rearrange("p (s c n) -> p s c n", s=2, c=NF)
        wf = pfx
        oh = h

        names = ("zb mk1 id1 cst tri1 gld th rld w_in0 w_in1 w_in2 w_in3 w_in4 w_in5 w_in6 w_in7 wh wl up uf uh ul "
                 "x_in c_in st1 st2 st3 zr1 zr2 z_ok zt_p ct_p z_hi z_lo c_hi c_lo vp v_hi v_lo qp q_hi q_lo kp k_hi k_lo "
                 "sp smk ex rc nm tp p_hi p_lo ov o_hi o_lo wp "
                 "xr_in f_x1 fs1 fs2 fs3 fr2 fy fyh fyl fsc fsb fp1 frk frs frs2 fpm fg fpt fptc fxs fms fr3 fh fp3 fh_hi fh_lo "
                 "fqk fv fq_hi fq_lo fv_hi f5p fT fsp fsm fex fpp fpf fpo frc fof fp9 fo_hi fo_lo fup fu fm2 fr4 fh2 fp11 "
                 "fh2_hi fh2_lo f12 fe fe3 fgl f13 fg_hi fg_lo fw3 fxp fx_hi fx_lo fsca ft1 fot out_d pool_passed dve_passed").split()
        s = {n: sem(n) for n in names}
        (zb, mk1, id1, cst, tri1, gld, th, rld, w_in0, w_in1, w_in2, w_in3, w_in4, w_in5, w_in6, w_in7, wh, wl, up, uf, uh, ul,
         x_in, c_in, st1, st2, st3, zr1, zr2, z_ok, zt_p, ct_p, z_hi, z_lo, c_hi, c_lo, vp, v_hi, v_lo, qp, q_hi, q_lo, kp,
         k_hi, k_lo, sp, smk, ex, rc, nm, tp, p_hi, p_lo, ov, o_hi, o_lo, wp,
         xr_in, f_x1, fs1, fs2, fs3, fr2, fy, fyh, fyl, fsc, fsb, fp1, frk, frs, frs2, fpm, fg, fpt, fptc, fxs, fms, fr3, fh, fp3,
         fh_hi, fh_lo, fqk, fv, fq_hi, fq_lo, fv_hi, f5p, fT, fsp, fsm, fex, fpp, fpf, fpo, frc, fof, fp9, fo_hi, fo_lo,
         fup, fu, fm2, fr4, fh2, fp11, fh2_hi, fh2_lo, f12, fe, fe3, fgl, f13, fg_hi, fg_lo, fw3, fxp, fx_hi,
         fx_lo, fsca, ft1, fot, out_d, pool_passed, dve_passed) = [s[n] for n in names]
        block = es.enter_context(nc.Block())

        tok = lambda t, b: t[b].rearrange("(t p) d -> p t d", p=P)
        raw_in = [
            (stage0[:, :].rearrange("p (c h e) -> p c h e", c=NC, h=H), Wq.rearrange("h (c p) e -> p c h e", p=P)),
            (stage1[:, :].rearrange("p (c h e) -> p c h e", c=NC, h=H), Wk.rearrange("h (c p) e -> p c h e", p=P)),
            (stage0[:, :].rearrange("p (c h e) -> p c h e", c=NC, h=H), Wv.rearrange("h (c p) e -> p c h e", p=P)),
            (stage0[:, :].rearrange("p (c d) -> p c d", c=HP), Wo.rearrange("(c p) d -> p c d", p=P)),
        ]
        raw_sem = [w_in0, w_in1, w_in2, w_in3]
        raw_src = [stage0[:, :], stage1[:, :], stage0[:, :], stage0[:, :]]
        split_dst = [w[:, :, :, :].rearrange("p s c n -> p s (c n)") for w in (wqX, wkX, wvX, woX)]

        units = []
        qkv_raw = stage0[:, 0:1536].rearrange("p (j d) -> p j d", j=6)
        out_raw = stage0[:, 1536:2048].rearrange("p (j d) -> p j d", j=2)
        w12_raw = stage0[:, 0:1536].rearrange("p (j d) -> p j d", j=NF)
        w3_raw = stage0[:, 0:2 * DFF].rearrange("p (j d) -> p j d", j=2)
        for c in range(NC):
            cs = slice(c * P, (c + 1) * P)
            units.append((4, [(j * P, P, qkv_raw[:, j, cs]) for j in (0, 1)], P, wqkvX[:, :, c, 0:256], g1c[:, c:c + 1], -0.25))
            units.append((4, [((j - 2) * P, P, qkv_raw[:, j, cs]) for j in (2, 3)], P, wqkvX[:, :, c, 256:512],
                          g1c[:, c:c + 1], 1.0))
            units.append((4, [((j - 4) * P, P, qkv_raw[:, j, cs]) for j in (4, 5)], P, wqkvX[:, :, c, 512:768],
                          g1c[:, c:c + 1], 1.0))
            units.append((4, [(j * P, P, out_raw[:, j, cs]) for j in (0, 1)], P, woutX[:, :, c, :], None, 1.0))
        for q, dst in ((5, w1X), (6, w2X)):
            for c in range(NC):
                cs = slice(c * P, (c + 1) * P)
                units.append((q, [(j * P, P, w12_raw[:, j, cs]) for j in range(4)], P, dst[:, :, c, 0:512],
                              g2c[:, c:c + 1], 1.0))
                units.append((q, [(0, P, w12_raw[:, 4, cs]), (P, FR, w12_raw[0:FR, 5, cs])], P, dst[:, :, c, 512:DFF],
                              g2c[:, c:c + 1], 1.0))
        for c in range(NF):
            rows = P if c < NF - 1 else FR
            units.append((7, [(j * P, P, w3_raw[:, j, c * P:c * P + rows]) for j in range(2)], rows,
                          w3X[0:rows, :, c, :], None, 0.5))
        NU = len(units)
        last_unit = {q: max(i for i, w in enumerate(units) if w[0] == q) for q in (4, 5, 6, 7)}
        raw_sems = {4: w_in4, 5: w_in5, 6: w_in6, 7: w_in7}
        unit_at = [list(range(sl * NU // 5, (sl + 1) * NU // 5)) for sl in range(5)] + [[]] * 3

        bkV = [bkQ, bkK]

        @block.sync
        def _(eng):
            def load(b):
                need(eng, zt_p, 1, b, 0)
                eng.dma_start(xin[:, :, :], tok(x, b)).then_inc(x_in, 16)
                need(eng, ct_p, 1, b, 0)
                eng.dma_start(cin[:, :, :], tok(ctx_in, b)).then_inc(c_in, 16)

            def store(b):
                need(eng, fot, 1, b, 1)
                eng.dma_start(tok(out, b), ot).then_inc(out_d, 16)

            def load_residual(b):
                need(eng, ft1, 2, b, 0)
                eng.dma_start(x1[:, :, :], tok(x, b)).then_inc(xr_in, 16)

            load(0)
            for q in (0, 1):
                for c in range(NC):
                    eng.dma_start(raw_in[q][0][:, c], raw_in[q][1][:, c]).then_inc(raw_sem[q], 16)
            eng.dma_start(gcol[:, 0:1], g_xattn.partition_broadcast(P)).then_inc(gld, 16)
            eng.dma_start(gcol[:, 1:2], g_ffn.partition_broadcast(P)).then_inc(gld, 16)
            eng.dma_start(wrow[:, :], w_router.partition_broadcast(P)).then_inc(gld, 16)
            eng.dma_start(g1c[:, :], g1.rearrange("(c p) -> p c", p=P), allow_slow_non_contiguous=True).then_inc(rld, 16)
            eng.dma_start(g2c[:, :], g2.rearrange("(c p) -> p c", p=P), allow_slow_non_contiguous=True).then_inc(rld, 16)
            load_residual(0)
            for q in (2, 3):
                eng.wait_ge(wl, 1 if q == 2 else 3)
                parts = NC if q == 2 else 1
                for c in range(parts):
                    d, w = (raw_in[q][0][:, c], raw_in[q][1][:, c]) if q == 2 else raw_in[q]
                    eng.dma_start(d, w).then_inc(raw_sem[q], 16)
            eng.wait_ge(wl, 4)
            eng.dma_start(qkv_raw, W_qkv.rearrange("(j p) d -> p j d", p=P)).then_inc(w_in4, 16)
            eng.dma_start(out_raw, W_out.rearrange("(j p) d -> p j d", p=P)).then_inc(w_in4, 16)
            for q, w, sm_ in ((5, W1, w_in5), (6, W2, w_in6)):
                eng.wait_ge(up, last_unit[q - 1] + 1)
                eng.dma_start(w12_raw[:, 0:NF - 1, :], w[0:(NF - 1) * P, :].rearrange("(j p) d -> p j d", p=P))\
                   .then_inc(sm_, 16)
                eng.dma_start(w12_raw[0:FR, NF - 1, :], w[(NF - 1) * P:DFF, :]).then_inc(sm_, 16)
            eng.wait_ge(up, last_unit[6] + 1)
            eng.dma_start(w3_raw, W3.rearrange("(j p) d -> p j d", p=P)).then_inc(w_in7, 16)

            def iteration(i):
                load(i + 1)
                store(i - 2)
                load_residual(i)

            load(1)
            load(2)
            load_residual(1)
            with eng.Fori(2, B - 1) as i:
                iteration(i)
            store(B - 3)
            load_residual(B - 1)
            store(B - 2)
            store(B - 1)
            eng.wait_ge(out_d, 16 * B)

        @block.gpsimd
        def _(eng):
            eng.memset(ident[:, :], 0.0).then_inc(zb, 1)
            eng.memset(mask[:, :], 0.0).then_inc(zb, 1)
            eng.memset(tri[:, :, :], 1.0).then_inc(zb, 1)
            eng.memset(f32(kX[:, :, :, :]), 0.0).then_inc(id1, 1)
            eng.wait_ge(zb, 3)
            eng.affine_select(out=ident[:, :], in_=ident[:, :], compare_op=ALU.not_equal, fill=1.0, base=0,
                              pattern=[[-1, P]], channel_multiplier=1).then_inc(id1, 1)
            eng.affine_select(out=mask[:, P:2 * P], in_=mask[:, P:2 * P], compare_op=ALU.is_ge, fill=BIG, base=0,
                              pattern=[[-1, P]], channel_multiplier=1).then_inc(mk1, 1)
            for t in range(NT):
                eng.affine_select(out=tri[:, t, :], in_=tri[:, t, :], compare_op=ALU.is_gt, fill=0.0, base=t * P,
                                  pattern=[[-1, S]], channel_multiplier=1).then_inc(tri1, 1)
            eng.iota(iota[:, :], pattern=[[1, P]], base=0, channel_multiplier=0,
                     allow_small_or_imprecise_dtypes=True).then_inc(cst, 1)
            eng.memset(mhalf[:, :], -0.5).then_inc(cst, 1)
            eng.wait_ge(cst, 2)

            def prep(b):
                need(eng, st3, 1, b, 1)
                eng.tensor_tensor(rs[:, :], ve[:, :], mhalf[:, :], ALU.pow).then_inc(zr1, 1)
                need_apart(eng, zr1, 1, b, 1, pool_passed)
                eng.tensor_scalar(rsn[:, :], rs[:, :], -0.125, 1.0, ALU.mult, ALU.mult).then_inc(zr2, 1)

            def normalise(b, p):
                blk = pm[:, p % 2, :]
                need_apart(eng, rc, 8, b, p + 1, pool_passed)
                for j, (o, w) in enumerate(((0, 128), (128, 128), (256, 256), (512, 256))):
                    eng.tensor_scalar(blk[:, o:o + w], blk[:, o:o + w], ri[:, p % 2, j:j + 1], 1.0, ALU.mult,
                                      ALU.mult).then_inc(nm, 1)

            def ln2(b):
                need(eng, fs3, 1, b, 1)
                eng.tensor_tensor(rs2[:, :], ve2[:, :], mhalf[:, :], ALU.pow).then_inc(fr2, 1)

            def rms1(b):
                need(eng, fms, 1, b, 1)
                eng.tensor_tensor(rr[:, 0:1], ms[:, 0:1], mhalf[:, 0:1], ALU.pow).then_inc(fr3, 1)

            def rms2(b):
                need(eng, fm2, 1, b, 1)
                eng.tensor_tensor(rr[:, 1:2], ms[:, 1:2], mhalf[:, 0:1], ALU.pow).then_inc(fr4, 1)

            def iteration(i, attn, main, ahead):
                for p in range(HP):
                    if attn:
                        normalise(i, p)
                    if p == 3 and main:
                        rms1(i - 1)
                    if p == 1 and main:
                        ln2(i - 1)
                    if p == 5 and ahead:
                        prep(i + 1)
                    if p == 7 and main:
                        rms2(i - 1)

            prep(0)
            iteration(0, True, False, True)
            iteration(1, True, True, True)
            with eng.Fori(2, B - 1) as i:
                iteration(i, True, True, True)
            iteration(B - 1, True, True, False)
            iteration(B, False, True, False)

        @block.tensor
        def _(eng):
            def product(dst, terms, start=True, stop=True):
                n = len(terms) * 3
                k = 0
                for lhs, rhs in terms:
                    for a, c in ((0, 0), (0, 1), (1, 0)):
                        mm = eng.matmul(dst, lhs(a), rhs(c), start=(start and k == 0), stop=(stop and k == n - 1))
                        k += 1
                return mm

            def prep_T(b):
                need(eng, z_ok, 2, b, 2)
                need(eng, q_lo, 8, b, 0)
                for c in range(NC):
                    for t in range(NT):
                        mm = eng.transpose(bkQ[:, c * S + t * P:c * S + t * P + P], xin[:, t, c * P:(c + 1) * P], ident[:, :])
                mm.then_inc(zt_p, 1)
                need(eng, c_in, 16, b, 16)
                need(eng, k_lo, 16, b, 0)
                for c in range(NC):
                    for t in range(NT):
                        mm = eng.transpose(bkK[:, c * S + t * P:c * S + t * P + P], cin[:, t, c * P:(c + 1) * P], ident[:, :])
                mm.then_inc(ct_p, 1)

            def proj(b, p):
                cols = slice(p * P, (p + 1) * P)
                if p == 0:
                    need(eng, z_lo, 1, b, 1)
                elif p in (2, 4):
                    need(eng, v_lo, 4, b, p - 1)
                else:
                    need(eng, q_lo, 8, b, p)
                product(bkQ[:, 0:S], [(lambda a, c=c: wqX[:, a, c, cols], lambda a, c=c: zX[:, a, c, :]) for c in range(NC)])\
                    .then_inc(qp, 1)
                if p == 0:
                    need(eng, c_lo, 1, b, 1)
                elif p in (3, 5):
                    need(eng, v_lo, 4, b, p - 1)
                else:
                    need(eng, k_lo, 16, b, 2 * p)
                product(bkK[:, 0:S], [(lambda a, c=c: wkX[:, a, c, cols], lambda a, c=c: cX[:, a, c, :]) for c in range(NC)])\
                    .then_inc(kp, 1)

            def v_proj(b, half, t):
                p = 2 * half + t + 1
                if t == 0:
                    need(eng, q_lo, 8, b, p + 1)
                else:
                    need(eng, k_lo, 16, b, 2 * p + 2)
                product(bkV[t][:, :], [(lambda a, c=c: cX[:, a, c, t * P:(t + 1) * P],
                                        lambda a, c=c: wvX[:, a, c, half * 512:half * 512 + 512]) for c in range(NC)])\
                    .then_inc(vp, 1)

            def scores(b, p):
                need(eng, q_lo, 8, b, p + 1)
                need(eng, k_lo, 16, b, 2 * p + 2)
                need(eng, smk, 32, b, 4 * p)
                need(eng, p_lo, 16, b, 2 * p - 2)
                if p == 2:
                    need(eng, f_x1, 2, b, 0)
                if p == 6:
                    need(eng, f_x1, 2, b, 1)
                for qt, dst in ((0, bkS0[:, 0:256].rearrange("p (h k) -> p h k", h=2)),
                                (1, bkS1[:, :].rearrange("p (h k) -> p h k", h=2))):
                    product(dst, [(lambda a: qX[:, a, qt * P:(qt + 1) * P], lambda a: kX[:, a, :, 0:(qt + 1) * P])])\
                        .then_inc(sp, 1)

            def p_T(b, p, more=True):
                blk = pm[:, p % 2, :]
                need(eng, nm, 32, b, 4 * p + 4)
                for hh in range(2):
                    eng.transpose(bkP[:, hh * S:hh * S + P], blk[:, hh * P:(hh + 1) * P], ident[:, :])
                    mm = eng.transpose(bkP[:, hh * S + P:(hh + 1) * S], blk[:, 256 + hh * S:256 + hh * S + P], ident[:, :])
                mm.then_inc(tp, 1)
                if more:
                    need(eng, smk, 32, b, 4 * p + 6)
                for hh in range(2):
                    mm = eng.transpose(bkS0[:, 256 + hh * P:256 + (hh + 1) * P], blk[:, 256 + hh * S + P:256 + (hh + 1) * S],
                                       ident[:, :])
                mm.then_inc(tp, 1)

            def pv(b, p):
                half, cols = p // 4, slice((p % 4) * P, (p % 4 + 1) * P)
                need(eng, p_lo, 16, b, 2 * p + 2)
                need(eng, v_lo, 4, b, 2 * half + 2)
                need(eng, o_lo, 16, b, 2 * p)
                o = bkO[:, :].rearrange("p (h q) -> p h q", h=2)
                product(o, [(lambda a: vX[:, a, half, 0, cols], lambda a: p0X[:, a, :, :])], stop=False)
                product(o[:, :, P:S], [(lambda a: vX[:, a, half, 1, cols], lambda a: p1X[:, a, :, :])], start=False)\
                    .then_inc(ov, 1)

            def wo(b, half, attn=True):
                need(eng, o_lo, 16, b, 8 * half + 8)
                if half == 0:
                    need(eng, smk, 32, b, 24)
                elif attn:
                    need(eng, smk, 32, b, 32 + 8)
                for t in range(NT):
                    mm = product(bkS1[:, t * D:(t + 1) * D],
                                 [(lambda a, c=c: oX[:, a, c, t * P:(t + 1) * P], lambda a, c=c: woX[:, a, half * 4 + c, :])
                                  for c in range(HP // 2)])
                mm.then_inc(wp, 1)

            def weight_unit(k):
                q, parts, rows, dst, scale, const = units[k]
                eng.wait_ge(raw_sems[q], 16 if q == 7 else 32)
                if k >= 2:
                    eng.wait_ge(uf, k - 1)
                bank = (bkA, bkB)[k % 2]
                for col, n, src in parts:
                    mm = eng.transpose(bank[0:rows, col:col + n], src, ident[0:n, 0:n])
                mm.then_inc(up, 1)

            def F1(b):
                need(eng, fsb, 2, b, 2)
                need(eng, fot, 1, b, 0)
                for t in range(NT):
                    mm = eng.transpose(bkB[:, t * P:(t + 1) * P], h[:, t * P:(t + 1) * P], ident[:, :])
                mm.then_inc(fp1, 1)

            def F2(b):
                need(eng, fpm, 2, b, 2)
                need(eng, fyl, 1, b, 1)
                k = 0
                for t in range(NT):
                    for a in range(2):
                        mm = eng.matmul(bkA[:, 0:D], perm[:, t, :], yX[:, a, t, :], start=(k == 0), stop=(k == 3))
                        k += 1
                mm.then_inc(fg, 1)
                for t in range(NT):
                    mm = eng.transpose(bkB[:, t * P:(t + 1) * P], f32(perm[:, t, :]), ident[:, :])
                mm.then_inc(fpt, 1)

            def F3(b):
                need(eng, fh, 1, b, 1)
                need(eng, fptc, 1, b, 1)
                for c in range(NC):
                    mm = eng.transpose(bkB[:, c * P:(c + 1) * P], h[:, c * P:(c + 1) * P], ident[:, :])
                mm.then_inc(fp3, 1)

            def F4(b):
                need(eng, fh_lo, 1, b, 1)
                product(bkA[:, :], [(lambda a, c=c: hX[:, a, c, :], lambda a, c=c: wqkvX[:, a, c, 0:512]) for c in range(NC)])\
                    .then_inc(fqk, 1)
                product(bkB[:, 0:D], [(lambda a, c=c: hX[:, a, c, :], lambda a, c=c: wqkvX[:, a, c, 512:768])
                                      for c in range(NC)]).then_inc(fv, 1)

            def F5(b, arrays):
                need(eng, fq_lo, 3, b, 3)
                need(eng, fv_hi, 1, b, 1)
                for a in arrays:
                    bank = (bkA, bkB, bkB)[a]
                    if a == 2:
                        need(eng, fT, 3, b, 2)
                    for t in range(4):
                        mm = eng.transpose(bank[:, t * P:(t + 1) * P],
                                           f32(qkp[:, a, 4 * t:4 * t + 4, :]).rearrange("p h e -> p (h e)"), ident[:, :])
                    mm.then_inc(f5p, 1)

            def F6(b, r):
                need(eng, fT, 3, b, 3)
                if r >= 2:
                    need(eng, fpf, 4, b, r - 1)
                bank = (bkB, bkA)[r % 2]
                rows = slice(32 * r, 32 * r + 32)
                for t in range(4):
                    for a in (1, 2):
                        mm = eng.matmul(bank[:, t * P:(t + 1) * P], qkT[rows, 0, t, :], qkT[rows, a, t, :],
                                        start=(a == 1), stop=(a == 2))
                mm.then_inc(fsp, 1)

            def F7(b, r):
                need(eng, fex, 16, b, 4 * r + 4)
                if r == 3:
                    need(eng, fof, 2, b, 1)
                bank = (bkB, bkA)[r % 2]
                for t in range(4):
                    mm = eng.transpose(bank[:, t * P:(t + 1) * P], sf[:, r % 2, t, :], ident[:, :])
                mm.then_inc(fpp, 1)

            def F8(b, g):
                need(eng, fpf, 4, b, 2 * g + 2)
                if g == 0:
                    need(eng, fsm, 16, b, 16)
                for r in (2 * g, 2 * g + 1):
                    for t in range(4):
                        hd = 4 * t + r
                        mm = eng.matmul(bkA[:, hd * FHD:(hd + 1) * FHD], pf[:, r % 2, t, :], vf[:, hd * FHD:(hd + 1) * FHD],
                                        start=True, stop=True)
                mm.then_inc(fpo, 1)

            def F9(b):
                need(eng, fof, 2, b, 2)
                for c in range(NC):
                    mm = eng.transpose(bkB[:, c * P:(c + 1) * P], oh[:, c * P:(c + 1) * P], ident[:, :])
                mm.then_inc(fp9, 1)

            def F10(b):
                need(eng, fo_lo, 1, b, 1)
                product(bkA[:, 0:D], [(lambda a, c=c: hX[:, a, c, :], lambda a, c=c: woutX[:, a, c, :]) for c in range(NC)])\
                    .then_inc(fup, 1)

            def F11(b):
                need(eng, fh2, 1, b, 1)
                for c in range(NC):
                    mm = eng.transpose(bkB[:, c * P:(c + 1) * P], h[:, c * P:(c + 1) * P], ident[:, :])
                mm.then_inc(fp11, 1)

            def F12(b, j):
                o, w = FCH[j]
                if j == 0:
                    need(eng, fh2_lo, 1, b, 1)
                else:
                    need(eng, fgl, 2, b, 1)
                product(bkA[:, 0:w], [(lambda a, c=c: hX[:, a, c, :], lambda a, c=c: w1X[:, a, c, o:o + w]) for c in range(NC)])
                product(bkB[:, 0:w], [(lambda a, c=c: hX[:, a, c, :], lambda a, c=c: w2X[:, a, c, o:o + w]) for c in range(NC)])\
                    .then_inc(f12, 1)

            def F13(b):
                need(eng, fgl, 2, b, 2)
                for c in range(4):
                    mm = eng.transpose(bkA[:, c * P:(c + 1) * P], gb[:, c * P:(c + 1) * P], ident[:, :])
                mm.then_inc(f13, 1)
                eng.transpose(bkB[:, 0:P], gb[:, 4 * P:5 * P], ident[:, :])
                eng.transpose(bkB[0:FR, P:2 * P], gb[:, 5 * P:DFF], ident[:, :]).then_inc(f13, 1)

            def F14(b):
                need(eng, fg_lo, 3, b, 3)
                rows = lambda c: P if c < NF - 1 else FR
                product(bkA[:, 0:D], [(lambda a, c=c: gX[0:rows(c), a, c, :], lambda a, c=c: w3X[0:rows(c), a, c, :])
                                      for c in range(NF)]).then_inc(fw3, 1)

            def F15(b):
                need(eng, fx_lo, 1, b, 1)
                for t in range(NT):
                    for a in range(2):
                        mm = eng.matmul(bkB[:, t * D:(t + 1) * D], permT[:, t * P:(t + 1) * P], xpX[:, a, :],
                                        start=(a == 0), stop=(a == 1))
                mm.then_inc(fsca, 1)

            def iteration(i, attn, before, main, tail, ahead, weights=False):
                for p in range(HP):
                    if attn:
                        scores(i, p)
                    if p < 7 and attn:
                        proj(i, p + 1)
                    if p == 7 and ahead:
                        prep_T(i + 1)
                    if p == 1 and tail:
                        F13(i - 2)
                    if p == 4 and main:
                        F3(i - 1)
                    if p == 5 and main:
                        F5(i - 1, (2,))
                    if p == 6 and main:
                        F6(i - 1, 2)
                    if p == 6 and main:
                        F6(i - 1, 3)
                    if p == 7 and main:
                        F8(i - 1, 1)
                    if p == 0 and tail:
                        F11(i - 2)
                    if p >= 2 and attn:
                        pv(i, p - 2)
                    if p < 2 and before:
                        pv(i - 1, HP - 2 + p)
                    if p >= 1 and attn:
                        p_T(i, p - 1)
                    if p == 0 and before:
                        p_T(i - 1, HP - 1, more=attn)
                    if p == 0 and tail:
                        F12(i - 2, 0)
                    if p == 1 and tail:
                        F14(i - 2)
                    if p == 3 and main:
                        F2(i - 1)
                    if p == 4 and main:
                        F4(i - 1)
                    if p == 5 and main:
                        F6(i - 1, 0)
                    if p == 5 and main:
                        F6(i - 1, 1)
                    if p == 6 and main:
                        F8(i - 1, 0)
                    if p == 7 and main:
                        F9(i - 1)
                    if p == 5 and weights:
                        eng.wait_ge(wl, 4)
                    if p == 5 and attn:
                        wo(i, 0)
                    if p == 1 and before:
                        wo(i - 1, 1, attn)
                    if p < 4 and attn:
                        v_proj(i, p // 2, p % 2)
                    if p == 7 and ahead:
                        proj(i + 1, 0)
                    if weights:
                        for k in unit_at[p]:
                            weight_unit(k)
                    if p == 0 and tail:
                        F12(i - 2, 1)
                    if p == 1 and tail:
                        F15(i - 2)
                    if p == 2 and main:
                        F1(i - 1)
                    if p == 4 and main:
                        F5(i - 1, (0, 1))
                    if p == 5 and main:
                        F7(i - 1, 0)
                    if p == 5 and main:
                        F7(i - 1, 1)
                    if p == 6 and main:
                        F7(i - 1, 2)
                    if p == 6 and main:
                        F7(i - 1, 3)
                    if p == 7 and main:
                        F10(i - 1)

            eng.wait_ge(id1, 2)
            prep_T(0)
            eng.wait_ge(wl, 2)
            proj(0, 0)
            eng.wait_ge(wl, 3)
            iteration(0, True, False, False, False, True, weights=True)
            eng.wait_ge(ul, NU)
            iteration(1, True, True, True, False, True)
            with eng.Fori(2, B - 1) as i:
                iteration(i, True, True, True, True, True)
            iteration(B - 1, True, True, True, True, False)
            iteration(B, False, True, True, True, False)
            iteration(B + 1, False, False, False, True, False)

        @block.scalar
        def _(eng):
            def high(dst, src, done):
                eng.activation(dst, src, ACT.Copy).then_inc(done, 1)

            def prep_hi(b):
                need(eng, zt_p, 1, b, 1)
                high(zX[:, 0, :, :], bkQ[:, :].rearrange("p (c s) -> p c s", c=NC), z_hi)
                need(eng, ct_p, 1, b, 1)
                high(cX[:, 0, :, :], bkK[:, :].rearrange("p (c s) -> p c s", c=NC), c_hi)

            def v_hi_(b, half, tiles=(0, 1)):
                for t in tiles:
                    need(eng, vp, 4, b, 2 * half + t + 1)
                    high(vX[:, 0, half, t, :], bkV[t][:, :], v_hi)

            def qk_hi(b, p):
                need(eng, qp, 8, b, p + 1)
                high(qX[:, 0, :], bkQ[:, 0:S], q_hi)
                need(eng, kp, 8, b, p + 1)
                for hh in range(2):
                    r = slice(64 * hh, 64 * hh + 64)
                    high(kX[r, 0, hh, :], bkK[r, 0:S], k_hi)

            def exp(b, p):
                blk = pm[:, p % 2, :]
                for j, (o, w) in enumerate(((0, 128), (128, 128), (256, 256), (512, 256))):
                    need(eng, smk, 32, b, 4 * p + j + 1)
                    eng.activation(blk[:, o:o + w], blk[:, o:o + w], ACT.Exp, bias=mn[:, p % 2, j:j + 1], scale=-1.0,
                                   accum_out=sm[:, p % 2, j:j + 1]).then_inc(ex, 1)

            def p_hi_(b, p):
                need(eng, tp, 16, b, 2 * p + 1)
                high(p0X[:, 0, :, :], bkP[:, :].rearrange("p (h q) -> p h q", h=2), p_hi)
                need(eng, tp, 16, b, 2 * p + 2)
                high(p1X[:, 0, :, :], bkS0[:, 256:512].rearrange("p (h q) -> p h q", h=2), p_hi)

            def o_hi_(b, p):
                need(eng, ov, 8, b, p + 1)
                for hh in range(2):
                    r = slice(64 * hh, 64 * hh + 64)
                    high(oX[r, 0, p % 4, :], bkO[r, hh * S:(hh + 1) * S], o_hi)

            def A0(b):
                need(eng, fy, 2, b, 2)
                high(yX[:, 0, :, :], y, fyh)

            def A2(b):
                need(eng, fg, 1, b, 1)
                eng.activation(xs, bkA[:, 0:D], ACT.Copy).then_inc(fxs, 1)
                need(eng, fpt, 1, b, 1)
                high(permT[:, :], bkB[:, 0:S], fptc)

            def hX_hi(src_ready, done):
                def go(b):
                    need(eng, src_ready, 1, b, 1)
                    high(hX[:, 0, :, :], bkB[:, 0:D].rearrange("p (c n) -> p c n", c=NC), done)
                return go

            A3, A9, A11 = hX_hi(fp3, fh_hi), hX_hi(fp9, fo_hi), hX_hi(fp11, fh2_hi)

            def A4(b):
                need(eng, fqk, 1, b, 1)
                q_ = bkA[:, 0:D].rearrange("p (h e) -> p h e", h=FH)
                k_ = bkA[:, D:2 * D].rearrange("p (h e) -> p h e", h=FH)
                high(qkp[:, 0, :, 0:16], q_, fq_hi)
                high(qkp[:, 1, :, 0:16], k_, fq_hi)
                high(qkp[:, 1, :, 16:32], k_, fq_hi)
                need(eng, fv, 1, b, 1)
                eng.activation(vf[:, :], bkB[:, 0:D], ACT.Copy).then_inc(fv_hi, 1)

            def A5(b, arrays):
                for a in arrays:
                    bank = (bkA, bkB, bkB)[a]
                    need(eng, f5p, 3, b, a + 1)
                    high(qkT[:, a, :, :], bank[:, :].rearrange("p (t n) -> p t n", t=4), fT)

            def A6(b, r):
                for t in range(4):
                    hd = 4 * t + r
                    need(eng, fsm, 16, b, 4 * r + t + 1)
                    eng.activation(sf[:, r % 2, t, :], sf[:, r % 2, t, :], ACT.Exp, bias=mf[:, hd:hd + 1], scale=-1.0,
                                   accum_out=sumf[:, hd:hd + 1]).then_inc(fex, 1)

            def A7(b, r):
                need(eng, fpp, 4, b, r + 1)
                bank = (bkB, bkA)[r % 2]
                eng.activation(pf[:, r % 2, :, :], bank[:, :].rearrange("p (t n) -> p t n", t=4), ACT.Copy).then_inc(fpf, 1)

            def A12(b, j):
                need(eng, f12, 2, b, j + 1)
                w = FCH[j][1]
                eng.activation(eb[:, 0:w], bkA[:, 0:w], ACT.Tanh, scale=0.5).then_inc(fe, 1)

            def A13(b):
                need(eng, f13, 2, b, 1)
                high(gX[:, 0, 0:4, :], bkA[:, :].rearrange("p (c n) -> p c n", c=4), fg_hi)
                need(eng, f13, 2, b, 2)
                high(gX[:, 0, 4, :], bkB[:, 0:P], fg_hi)
                high(gX[0:FR, 0, 5, :], bkB[0:FR, P:2 * P], fg_hi)

            def A14(b):
                need(eng, fxp, 1, b, 1)
                high(xpX[:, 0, :], h[:, :], fx_hi)

            def weight_hi(k):
                rows, dst = units[k][2], units[k][3]
                w = dst.shape[-1]
                eng.wait_ge(uf, k + 1)
                high(dst[:, 0, :], wf[0:rows, 0:w], uh)

            def iteration(i, attn, before, main, tail, ahead, weights=False):
                for p in range(HP):
                    if p < 7 and attn:
                        qk_hi(i, p + 1)
                    if p == 7 and ahead:
                        prep_hi(i + 1)
                    if p == 1 and tail:
                        A13(i - 2)
                    if p == 4 and main:
                        A3(i - 1)
                    if p == 5 and main:
                        A5(i - 1, (2,))
                    if p == 0 and tail:
                        A11(i - 2)
                    if attn:
                        exp(i, p)
                    if p >= 2 and attn:
                        o_hi_(i, p - 2)
                    if p < 2 and before:
                        o_hi_(i - 1, HP - 2 + p)
                    if p >= 1 and attn:
                        p_hi_(i, p - 1)
                    if p == 0 and before:
                        p_hi_(i - 1, HP - 1)
                    if p == 6 and main:
                        A6(i - 1, 2)
                    if p == 6 and main:
                        A6(i - 1, 3)
                    if p == 0 and tail:
                        A12(i - 2, 0)
                    if p == 1 and tail:
                        A14(i - 2)
                    if p == 2 and main:
                        A0(i - 1)
                    if p == 3 and main:
                        A2(i - 1)
                    if p == 4 and main:
                        A4(i - 1)
                    if p == 7 and main:
                        A9(i - 1)
                    if p == 5 and main:
                        A6(i - 1, 0)
                    if p == 5 and main:
                        A6(i - 1, 1)
                    if p < 4 and attn:
                        v_hi_(i, p // 2, (p % 2,))
                    if p == 7 and ahead:
                        qk_hi(i + 1, 0)
                    if weights:
                        for k in unit_at[p]:
                            weight_hi(k)
                    if p == 0 and tail:
                        A12(i - 2, 1)
                    if p == 4 and main:
                        A5(i - 1, (0, 1))
                    if p == 5 and main:
                        A7(i - 1, 0)
                    if p == 5 and main:
                        A7(i - 1, 1)
                    if p == 6 and main:
                        A7(i - 1, 2)
                    if p == 6 and main:
                        A7(i - 1, 3)

            eng.wait_ge(gld, 48)
            eng.activation(tg[:, :], gcol[:, :], ACT.Tanh).then_inc(th, 1)
            for q in (0, 1):
                eng.wait_ge(raw_sem[q], 32)
                high(split_dst[q][:, 0, :], raw_src[q], wh)
            prep_hi(0)
            eng.wait_ge(raw_sem[2], 32)
            high(split_dst[2][:, 0, :], raw_src[2], wh)
            qk_hi(0, 0)
            eng.wait_ge(raw_sem[3], 16)
            high(split_dst[3][:, 0, :], raw_src[3], wh)
            iteration(0, True, False, False, False, True, weights=True)
            iteration(1, True, True, True, False, True)
            with eng.Fori(2, B - 1) as i:
                iteration(i, True, True, True, True, True)
            iteration(B - 1, True, True, True, True, False)
            iteration(B, False, True, True, True, False)
            iteration(B + 1, False, False, False, True, False)

        @block.vector
        def _(eng):
            def low(dst, src, hi, done):
                eng.tensor_tensor(dst, src, f32(hi), ALU.subtract).then_inc(done, 1)

            def prep_stats(b):
                need(eng, x_in, 16, b, 16)
                for t in range(NT):
                    eng.bn_stats(bst[:, t, :], xin[:, t, :]).then_inc(st1, 1)
                need_apart(eng, st1, 2, b, 2, dve_passed)
                for t in range(NT):
                    eng.bn_aggr(mv[:, t, :], bst[:, t, :]).then_inc(st2, 1)
                need(eng, st2, 2, b, 2)
                eng.tensor_scalar(ve[:, :], mv[:, :, 1], 1e-5, None, ALU.add).then_inc(st3, 1)

            def prep_z(b):
                need(eng, zr2, 1, b, 1)
                for t in range(NT):
                    eng.tensor_scalar(xin[:, t, :], xin[:, t, :], mv[:, t, 0:1], rsn[:, t:t + 1], ALU.subtract, ALU.mult)\
                       .then_inc(z_ok, 1)

            def prep_lo(b):
                need(eng, z_hi, 1, b, 1)
                low(zX[:, 1, :, :], bkQ[:, :].rearrange("p (c s) -> p c s", c=NC), zX[:, 0, :, :], z_lo)
                need(eng, c_hi, 1, b, 1)
                low(cX[:, 1, :, :], bkK[:, :].rearrange("p (c s) -> p c s", c=NC), cX[:, 0, :, :], c_lo)

            def v_lo_(b, half, tiles=(0, 1)):
                for t in tiles:
                    need(eng, v_hi, 4, b, 2 * half + t + 1)
                    low(vX[:, 1, half, t, :], bkV[t][:, :], vX[:, 0, half, t, :], v_lo)

            def qk_lo(b, p):
                need(eng, q_hi, 8, b, p + 1)
                low(qX[:, 1, :], bkQ[:, 0:S], qX[:, 0, :], q_lo)
                need(eng, k_hi, 16, b, 2 * p + 2)
                for hh in range(2):
                    r = slice(64 * hh, 64 * hh + 64)
                    low(kX[r, 1, hh, :], bkK[r, 0:S], kX[r, 0, hh, :], k_lo)

            def mask_min(b, p):
                blk = pm[:, p % 2, :]
                for j, (o, w) in enumerate(((0, 128), (128, 128), (256, 256), (512, 256))):
                    src = bkS0[:, j * P:(j + 1) * P] if j < 2 else bkS1[:, (j - 2) * S:(j - 1) * S]
                    if j in (0, 2):
                        need_apart(eng, sp, 16, b, 2 * p + (1 if j < 2 else 2), dve_passed)
                    eng.tensor_tensor_reduce(blk[:, o:o + w], src, mask[:, 2 * P - w:2 * P], 1.0, 3e38, ALU.add, ALU.min,
                                             mn[:, p % 2, j:j + 1]).then_inc(smk, 1)

            def recip(b, p):
                need(eng, ex, 32, b, 4 * p + 4)
                eng.reciprocal(ri[:, p % 2, :], sm[:, p % 2, :]).then_inc(rc, 1)

            def p_lo_(b, p):
                need(eng, p_hi, 16, b, 2 * p + 1)
                low(p0X[:, 1, :, :], bkP[:, :].rearrange("p (h q) -> p h q", h=2), p0X[:, 0, :, :], p_lo)
                need(eng, p_hi, 16, b, 2 * p + 2)
                low(p1X[:, 1, :, :], bkS0[:, 256:512].rearrange("p (h q) -> p h q", h=2), p1X[:, 0, :, :], p_lo)

            def o_lo_(b, p):
                need(eng, o_hi, 16, b, 2 * p + 2)
                for hh in range(2):
                    r = slice(64 * hh, 64 * hh + 64)
                    low(oX[r, 1, p % 4, :], bkO[r, hh * S:(hh + 1) * S], oX[r, 0, p % 4, :], o_lo)

            wo_out = bkS1[:, :].rearrange("p (t d) -> p t d", t=NT)

            def add_wo(b, half):
                need(eng, wp, 2, b, half + 1)
                if half == 0:
                    need(eng, xr_in, 16, b, 16)
                else:
                    need(eng, f_x1, 2, b, 1)
                eng.scalar_tensor_tensor(out=x1[:, :, :], in0=wo_out, scalar=tg[:, 0:1], in1=x1[:, :, :], op0=ALU.mult,
                                         op1=ALU.add).then_inc(f_x1, 1)

            def V0a(b):
                need(eng, f_x1, 2, b, 2)
                for t in range(NT):
                    eng.bn_stats(bst2[:, t, :], x1[:, t, :]).then_inc(fs1, 1)
                need_apart(eng, fs1, 2, b, 2, dve_passed)
                for t in range(NT):
                    eng.bn_aggr(mv2[:, t, :], bst2[:, t, :]).then_inc(fs2, 1)
                need(eng, fs2, 2, b, 2)
                eng.tensor_scalar(ve2[:, :], mv2[:, :, 1], 1e-5, None, ALU.add).then_inc(fs3, 1)

            def V0b(b):
                need(eng, fr2, 1, b, 1)
                for t in range(NT):
                    eng.tensor_scalar(y[:, t, :], x1[:, t, :], mv2[:, t, 0:1], rs2[:, t:t + 1], ALU.subtract, ALU.mult)\
                       .then_inc(fy, 1)
                need(eng, fy, 2, b, 2)
                for t in range(NT):
                    eng.tensor_tensor_reduce(junk[:, t, :], y[:, t, :], wrow[:, :], 1.0, 0.0, ALU.mult, ALU.add, sc[:, t:t + 1])\
                       .then_inc(fsc, 1)
                need(eng, fsc, 2, b, 2)
                for t in range(NT):
                    eng.tensor_scalar(h[:, t * P:(t + 1) * P], mask[:, 0:P], sc[:, t:t + 1], None, ALU.add).then_inc(fsb, 1)

            def V0c(b):
                need(eng, fyh, 1, b, 1)
                low(yX[:, 1, :, :], y, yX[:, 0, :, :], fyl)

            def V1(b):
                need(eng, fp1, 1, b, 1)
                for t in range(NT):
                    eng.tensor_scalar(junk[:, 2 * t, :], bkB[:, 0:S], sc[:, t:t + 1], None, ALU.is_gt, ALU.add,
                                      accum_out=ra[:, t:t + 1]).then_inc(frk, 1)
                    eng.scalar_tensor_tensor(out=junk[:, 2 * t + 1, :], in0=bkB[:, 0:S], scalar=sc[:, t:t + 1], in1=tri[:, t, :],
                                             op0=ALU.is_equal, op1=ALU.mult, accum_out=rb[:, t:t + 1]).then_inc(frk, 1)
                need(eng, frk, 4, b, 4)
                eng.tensor_tensor(rank[:, :], ra[:, :], rb[:, :], ALU.add).then_inc(frs, 1)
                need(eng, frs, 1, b, 1)
                for t in range(NT):
                    eng.tensor_scalar(perm[:, t, :], iota[:, :], rank[:, t:t + 1], None, ALU.is_equal).then_inc(fpm, 1)

            def V2(b):
                eng.tensor_scalar(nst[:, :], rank[:, :], float(CAP), tg[:, 1:2], ALU.is_ge, ALU.mult).then_inc(frs2, 1)
                need(eng, fxs, 1, b, 1)
                eng.tensor_tensor_reduce(h[:, :], xs, xs, 1.0 / D, 1e-6, ALU.mult, ALU.add, ms[:, 0:1]).then_inc(fms, 1)
                need(eng, frs2, 1, b, 1)
                need(eng, out_d, 16, b, 0)
                for t in range(NT):
                    eng.scalar_tensor_tensor(out=ot[:, t, :], in0=y[:, t, :], scalar=nst[:, t:t + 1], in1=x1[:, t, :],
                                             op0=ALU.mult, op1=ALU.add).then_inc(ft1, 1)

            def V2b(b):
                need(eng, fr3, 1, b, 1)
                eng.tensor_scalar(h[:, :], xs, rr[:, 0:1], None, ALU.mult).then_inc(fh, 1)

            def hX_lo(src_ready, done):
                def go(b):
                    need(eng, src_ready, 1, b, 1)
                    low(hX[:, 1, :, :], bkB[:, 0:D].rearrange("p (c n) -> p c n", c=NC), hX[:, 0, :, :], done)
                return go

            V3, V9, V11 = hX_lo(fh_hi, fh_lo), hX_lo(fo_hi, fo_lo), hX_lo(fh2_hi, fh2_lo)

            def V4(b):
                need(eng, fq_hi, 3, b, 3)
                q_ = bkA[:, 0:D].rearrange("p (h e) -> p h e", h=FH)
                k_ = bkA[:, D:2 * D].rearrange("p (h e) -> p h e", h=FH)
                low(qkp[:, 0, :, 16:32], q_, qkp[:, 0, :, 0:16], fq_lo)
                low(qkp[:, 2, :, 0:16], k_, qkp[:, 1, :, 0:16], fq_lo)
                low(qkp[:, 2, :, 16:32], k_, qkp[:, 1, :, 0:16], fq_lo)

            def V6(b, r):
                need_apart(eng, fsp, 4, b, r + 1, dve_passed)
                bank = (bkB, bkA)[r % 2]
                for t in range(4):
                    hd = 4 * t + r
                    eng.tensor_tensor_reduce(sf[:, r % 2, t, :], bank[:, t * P:(t + 1) * P], mask[:, P:2 * P], 1.0, 3e38,
                                             ALU.add, ALU.min, mf[:, hd:hd + 1]).then_inc(fsm, 1)

            def V8(b, g):
                need(eng, fex, 16, b, 8 * g + 8)
                rv = rif[:, :].rearrange("p (t r) -> p t r", r=4)[:, :, 2 * g:2 * g + 2]
                eng.reciprocal(rv, sumf[:, :].rearrange("p (t r) -> p t r", r=4)[:, :, 2 * g:2 * g + 2]).then_inc(frc, 1)
                need(eng, frc, 2, b, g + 1)
                need(eng, fpo, 2, b, g + 1)
                po = bkA[:, 0:D].rearrange("p (t r e) -> p t r e", t=4, r=4)[:, :, 2 * g:2 * g + 2, :]
                oo = oh[:, :].rearrange("p (t r e) -> p t r e", t=4, r=4)[:, :, 2 * g:2 * g + 2, :]
                eng.tensor_tensor(oo, po, rv.unsqueeze(3).to_broadcast([P, 4, 2, FHD]), ALU.mult).then_inc(fof, 1)

            def V10(b):
                need(eng, fup, 1, b, 1)
                eng.tensor_tensor(u, bkA[:, 0:D], xs, ALU.add).then_inc(fu, 1)
                need(eng, fu, 1, b, 1)
                eng.tensor_tensor_reduce(h[:, :], u, u, 1.0 / D, 1e-6, ALU.mult, ALU.add, ms[:, 1:2]).then_inc(fm2, 1)
                need(eng, fr4, 1, b, 1)
                eng.tensor_scalar(h[:, :], u, rr[:, 1:2], None, ALU.mult).then_inc(fh2, 1)

            def V12(b, j):
                o, w = FCH[j]
                need(eng, fe, 2, b, j + 1)
                eng.scalar_tensor_tensor(out=eb[:, 0:w], in0=eb[:, 0:w], scalar=1.0, in1=bkA[:, 0:w], op0=ALU.add,
                                         op1=ALU.mult).then_inc(fe3, 1)
                need(eng, fe3, 2, b, j + 1)
                eng.tensor_tensor(gb[:, o:o + w], bkB[:, 0:w], eb[:, 0:w], ALU.mult).then_inc(fgl, 1)

            def V13(b):
                need(eng, fg_hi, 3, b, 1)
                low(gX[:, 1, 0:4, :], bkA[:, :].rearrange("p (c n) -> p c n", c=4), gX[:, 0, 0:4, :], fg_lo)
                need(eng, fg_hi, 3, b, 3)
                low(gX[:, 1, 4, :], bkB[:, 0:P], gX[:, 0, 4, :], fg_lo)
                low(gX[0:FR, 1, 5, :], bkB[0:FR, P:2 * P], gX[0:FR, 0, 5, :], fg_lo)

            def V14(b):
                need(eng, fw3, 1, b, 1)
                eng.tensor_tensor(h[:, :], bkA[:, 0:D], u, ALU.add).then_inc(fxp, 1)
                need(eng, fx_hi, 1, b, 1)
                low(xpX[:, 1, :], h[:, :], xpX[:, 0, :], fx_lo)

            def V15(b):
                need(eng, fsca, 1, b, 1)
                eng.scalar_tensor_tensor(out=ot, in0=bkB[:, :].rearrange("p (t d) -> p t d", t=NT), scalar=tg[:, 1:2], in1=ot,
                                         op0=ALU.mult, op1=ALU.add).then_inc(fot, 1)

            def weight_lo(k):
                q, parts, rows, dst, scale, const = units[k]
                w = dst.shape[-1]
                bank = (bkA, bkB)[k % 2]
                eng.wait_ge(up, k + 1)
                if k >= 1:
                    eng.wait_ge(uh, k)
                    eng.wait_ge(ul, k)
                eng.tensor_scalar(wf[0:rows, 0:w], bank[0:rows, 0:w], const if scale is None else scale,
                                  1.0 if scale is None else const, ALU.mult, ALU.mult).then_inc(uf, 1)
                eng.wait_ge(uh, k + 1)
                low(dst[:, 1, :], wf[0:rows, 0:w], dst[:, 0, :], ul)

            def iteration(i, attn, before, main, tail, ahead, weights=False):
                for p in range(HP):
                    if attn:
                        mask_min(i, p)
                    if p < 7 and attn:
                        qk_lo(i, p + 1)
                    if p == 7 and ahead:
                        prep_lo(i + 1)
                    if p == 1 and tail:
                        V13(i - 2)
                    if p == 2 and main:
                        V0b(i - 1)
                    if p == 4 and main:
                        V3(i - 1)
                    if p == 6 and main:
                        V6(i - 1, 2)
                    if p == 6 and main:
                        V6(i - 1, 3)
                    if p == 7 and main:
                        V8(i - 1, 1)
                    if p == 0 and tail:
                        V11(i - 2)
                    if p >= 2 and attn:
                        o_lo_(i, p - 2)
                    if p < 2 and before:
                        o_lo_(i - 1, HP - 2 + p)
                    if p >= 1 and attn:
                        p_lo_(i, p - 1)
                    if p == 0 and before:
                        p_lo_(i - 1, HP - 1)
                    if attn:
                        recip(i, p)
                    if p == 0 and tail:
                        V12(i - 2, 0)
                    if p == 1 and tail:
                        V14(i - 2)
                    if p == 2 and main:
                        V0c(i - 1)
                    if p == 3 and main:
                        V2(i - 1)
                    if p == 4 and main:
                        V4(i - 1)
                    if p == 5 and main:
                        V6(i - 1, 0)
                    if p == 5 and main:
                        V6(i - 1, 1)
                    if p == 6 and main:
                        V8(i - 1, 0)
                    if p == 7 and main:
                        V9(i - 1)
                    if p == 5 and attn:
                        add_wo(i, 0)
                    if p == 1 and before:
                        add_wo(i - 1, 1)
                    if p < 4 and attn:
                        v_lo_(i, p // 2, (p % 2,))
                    if p == 7 and ahead:
                        qk_lo(i + 1, 0)
                    if weights:
                        for k in unit_at[p]:
                            weight_lo(k)
                    if p == 0 and tail:
                        V12(i - 2, 1)
                    if p == 1 and tail:
                        V15(i - 2)
                    if p == 1 and before:
                        V0a(i - 1)
                    if p == 2 and main:
                        V1(i - 1)
                    if p == 3 and main:
                        V2b(i - 1)
                    if p == 5 and ahead:
                        prep_stats(i + 1)
                    if p == 6 and ahead:
                        prep_z(i + 1)
                    if p == 7 and main:
                        V10(i - 1)

            eng.wait_ge(mk1, 1)
            eng.wait_ge(tri1, NT)
            eng.wait_ge(cst, 2)
            prep_stats(0)
            prep_z(0)
            for q in (0, 1):
                eng.wait_ge(wh, q + 1)
                low(split_dst[q][:, 1, :], raw_src[q], split_dst[q][:, 0, :], wl)
            prep_lo(0)
            eng.wait_ge(wh, 3)
            low(split_dst[2][:, 1, :], raw_src[2], split_dst[2][:, 0, :], wl)
            qk_lo(0, 0)
            eng.wait_ge(wh, 4)
            low(split_dst[3][:, 1, :], raw_src[3], split_dst[3][:, 0, :], wl)
            eng.wait_ge(gld, 48)
            eng.wait_ge(rld, 32)
            eng.wait_ge(th, 1)
            iteration(0, True, False, False, False, True, weights=True)
            iteration(1, True, True, True, False, True)
            with eng.Fori(2, B - 1) as i:
                iteration(i, True, True, True, True, True)
            iteration(B - 1, True, True, True, True, False)
            iteration(B, False, True, True, True, False)
            iteration(B + 1, False, False, False, True, False)


_INS = ["x", "ctx_1024", "g_xattn", "g_ffn", "L0_xattn_Wq", "L0_xattn_Wk", "L0_xattn_Wv", "L0_xattn_Wo",
        "L0_ffn_w_router", "L0_ffn_W_qkv", "L0_ffn_W_out", "L0_ffn_g1", "L0_ffn_g2", "L0_ffn_W1", "L0_ffn_W2", "L0_ffn_W3"]


def kernel(**inputs):
    import numpy as np
    import concourse.bacc as bacc
    from concourse import mybir as mb
    from concourse.bass_utils import run_bass_kernel_spmd as run

    nc = bacc.Bacc("TRN2", target_bir_lowering=False, num_devices=1)
    arrays, args = {}, []
    for name in _INS:
        a = np.ascontiguousarray(inputs[name])
        arrays[f"in_{name}"] = a
        args.append(nc.dram_tensor(f"in_{name}", a.shape, mb.dt.from_np(a.dtype), kind="ExternalInput").ap())
    out = nc.dram_tensor("out_0", (B, S, D), mb.dt.float32, kind="ExternalOutput").ap()
    build(nc, *args, out)
    return run(nc, [arrays], core_ids=[0]).results[0]["out_0"]
```

```python
from contextlib import ExitStack

import concourse.bass as bass
from concourse import mybir

ALU = mybir.AluOpType
ACT = mybir.ActivationFunctionType
F32 = mybir.dt.float32
F32R = mybir.dt.float32r
BF16 = mybir.dt.bfloat16

P = 128
B, S, D = 16, 256, 256
H, HD = 16, 64
NT = S // P
NC = D // P
HP = H // 2
CAP = 128
FH, FHD = 16, 16
DFF = D * 4 * 2 // 3
NF = (DFF + P - 1) // P
FR = DFF - (NF - 1) * P
FCH = [(0, 342), (342, DFF - 342)]
BIG = 1e30
PM_BLOCKS = ((2, 256, 256), (3, 512, 256), (0, 0, 128), (1, 128, 128))
W_NEED = {0: 3, 3: 6, 5: 8}
V_SLOT = {0: ((0, 0),), 1: ((0, 1),), 3: ((1, 0),), 4: ((1, 1),)}


def need(eng, sem, per, b, c):
    v = b * per + c
    if isinstance(v, int) and v <= 0:
        return
    eng.wait_ge(sem, v)


def need_apart(eng, sem, per, b, c, passed):
    need(eng, sem, per, b, c)
    if not isinstance(b, int):
        eng.sem_inc(passed, 1)


def f32(ap):
    return ap.bitcast(F32)


def build(nc, x, ctx_in, g_xattn, g_ffn, Wq, Wk, Wv, Wo, w_router, W_qkv, W_out, g1, g2, W1, W2, W3, out):
    with ExitStack() as es:
        def sb(name, shape, dt=F32):
            return es.enter_context(nc.sbuf_tensor(name, shape, dt))

        def sem(name):
            return es.enter_context(nc.semaphore(name))

        bkQ = es.enter_context(nc.psum_tensor("bkQ", [P, 512], F32))
        bkK = es.enter_context(nc.psum_tensor("bkK", [P, 512], F32))
        bkS1 = es.enter_context(nc.psum_tensor("bkS1", [P, 512], F32))
        bkS0 = es.enter_context(nc.psum_tensor("bkS0", [P, 512], F32))
        bkP = es.enter_context(nc.psum_tensor("bkP", [P, 512], F32))
        bkO = es.enter_context(nc.psum_tensor("bkO", [P, 512], F32))
        bkA = es.enter_context(nc.psum_tensor("bkA", [P, 512], F32))
        bkB = es.enter_context(nc.psum_tensor("bkB", [P, 512], F32))

        ident = sb("ident", [P, P])
        mask = sb("mask", [P, 2 * P], BF16)
        tri = sb("tri", [P, NT, S], BF16)
        iota = sb("iota", [P, P])
        wrow = sb("wrow", [P, D])
        mhalf = sb("mhalf", [P, NT])
        gcol = sb("gcol", [P, 2])
        tg = sb("tg", [P, 2])
        gains = sb("gains", [P, 3 * NC + 1])
        g1c = gains[:, 0:NC]
        g2c = gains[:, NC:2 * NC]
        g1q = gains[:, 2 * NC:3 * NC]
        half_col = gains[:, 3 * NC:3 * NC + 1]

        with nc.sbuf_tensor("raw", [P, 8 * 1024], F32) as raw_head:
            pass

        w1X = sb("w1X", [P, 2, NC, DFF], F32R)
        w2X = sb("w2X", [P, 2, NC, DFF], F32R)
        w3X = sb("w3X", [P, 2, NF, D], F32R)
        wqX = sb("wqX", [P, 2, NC, H * HD], F32R)
        wkX = sb("wkX", [P, 2, NC, H * HD], F32R)
        wvX = sb("wvX", [P, 2, NC, H * HD], F32R)
        woX = sb("woX", [P, 2, HP, D], F32R)
        wqkvX = sb("wqkvX", [P, 2, NC, 3 * D], F32R)
        woutX = sb("woutX", [P, 2, NC, D], F32R)

        xin = sb("xin", [P, NT, D])
        cin = sb("cin", [P, NT, D])
        zX = sb("zX", [P, 2, NC, S], F32R)
        cX = sb("cX", [P, 2, NC, S], F32R)
        vX = sb("vX", [P, 2, 2, NT, 512], F32R)
        qX = sb("qX", [P, 2, S], F32R)
        kX = sb("kX", [P, 2, 2, S], F32R)
        pm = sb("pm", [P, 2, 768])
        p0X = sb("p0X", [P, 2, 2, S], F32R)
        p1X = sb("p1X", [P, 2, 2, P], F32R)
        oX = sb("oX", [P, 2, HP // 2, S], F32R)
        bst = sb("bst", [P, NT, 6])
        mv = sb("mv", [P, NT, 2])
        ve = sb("ve", [P, NT])
        rs = sb("rs", [P, NT])
        rsn = sb("rsn", [P, NT])
        mn = sb("mn", [P, 2, 4])
        sm = sb("sm", [P, 2, 4])
        ri = sb("ri", [P, 2, 4])

        x1 = sb("x1", [P, NT, D])
        stage1 = sb("stage1", [P, 2048])
        y = stage1[:, 0:512].rearrange("p (t d) -> p t d", t=NT)
        xs = stage1[:, 512:768]
        u = stage1[:, 768:1024]
        ot = stage1[:, 1024:1536].rearrange("p (t d) -> p t d", t=NT)
        h = sb("h", [P, D])
        bst2 = sb("bst2", [P, NT, 6])
        mv2 = sb("mv2", [P, NT, 2])
        ve2 = sb("ve2", [P, NT])
        rs2 = sb("rs2", [P, NT])
        sc = sb("sc", [P, NT])
        junk = stage1[:, 1536:2048].bitcast(BF16).rearrange("p (j n) -> p j n", j=4)
        ra = sb("ra", [P, NT])
        rb = sb("rb", [P, NT])
        rank = sb("rank", [P, NT])
        nst = sb("nst", [P, NT])
        ms = sb("ms", [P, 2])
        rr = sb("rr", [P, 2])
        perm = sb("perm", [P, NT, P], F32R)
        permT = sb("permT", [P, S], F32R)
        hX = sb("hX", [P, 2, NC, P], F32R)
        r1X = sb("r1X", [P, 1536], F32R)
        r2X = sb("r2X", [P, 1536], F32R)
        vf = sb("vf", [P, D])
        stage0 = sb("stage0", [P, 2048])
        sf = stage0[:, 0:1024].rearrange("p (r t k) -> p r t k", r=2, t=4)
        pf = stage0[:, 1024:2048].rearrange("p (r t k) -> p r t k", r=2, t=4)
        gb = stage0[:, 0:DFF]
        eb = stage0[:, 1024:1024 + 342]
        mf = sb("mf", [P, FH])
        sumf = sb("sumf", [P, FH])
        rif = sb("rif", [P, FH])
        yX = r2X[:, 0:1024].rearrange("p (s t d) -> p s t d", s=2, t=NT)
        qkp = r2X[:, :].rearrange("p (a h e) -> p a h e", a=3, h=FH)
        xpX = r2X[:, 1024:1536].rearrange("p (s d) -> p s d", s=2)
        qkT = r1X[:, :].rearrange("p (a t n) -> p a t n", a=3, t=4)
        gX = r1X[:, :].rearrange("p (s c n) -> p s c n", s=2, c=NF)
        oh = h

        names = ("zb mk1 id1 cst tri1 gld th rld w_q0 w_k0 w_v0 w_q1 w_k1 w_v1 w_o0 w_o1 gsc w_in4 w_in5 w_in6 w_in7 wh wl up uh ul "
                 "x_in c_in st1 st2 st3 zr1 zr2 z_ok zt_p ct_p z_hi z_lo c_hi c_lo vp v_hi v_lo qp q_hi q_lo kp k_hi k_lo "
                 "sp smk ex rc nm tp p_hi p_lo ov o_hi o_lo wp "
                 "xr_in f_x1 fs1 fs2 fs3 fr2 fy fyh fyl fsc fp1 frk frs frs2 fpm fg fpt fptc fxs fms fr3 fh fp3 fh_hi fh_lo "
                 "fqk fv fq_hi fq_lo fv_hi f5p fT fsp fsm fex fpp fpf fpo frc fof fp9 fo_hi fo_lo fup fu fm2 fr4 fh2 fp11 "
                 "fh2_hi fh2_lo f12 fe fe3 fgl f13 fg_hi fg_lo fw3 fxp fx_hi fx_lo fsca fky ft1 fot out_d pool_passed dve_passed").split()
        s = {n: sem(n) for n in names}
        (zb, mk1, id1, cst, tri1, gld, th, rld, w_q0, w_k0, w_v0, w_q1, w_k1, w_v1, w_o0, w_o1, gsc, w_in4, w_in5, w_in6, w_in7, wh, wl, up, uh, ul,
         x_in, c_in, st1, st2, st3, zr1, zr2, z_ok, zt_p, ct_p, z_hi, z_lo, c_hi, c_lo, vp, v_hi, v_lo, qp, q_hi, q_lo, kp,
         k_hi, k_lo, sp, smk, ex, rc, nm, tp, p_hi, p_lo, ov, o_hi, o_lo, wp,
         xr_in, f_x1, fs1, fs2, fs3, fr2, fy, fyh, fyl, fsc, fp1, frk, frs, frs2, fpm, fg, fpt, fptc, fxs, fms, fr3, fh, fp3,
         fh_hi, fh_lo, fqk, fv, fq_hi, fq_lo, fv_hi, f5p, fT, fsp, fsm, fex, fpp, fpf, fpo, frc, fof, fp9, fo_hi, fo_lo,
         fup, fu, fm2, fr4, fh2, fp11, fh2_hi, fh2_lo, f12, fe, fe3, fgl, f13, fg_hi, fg_lo, fw3, fxp, fx_hi,
         fx_lo, fsca, fky, ft1, fot, out_d, pool_passed, dve_passed) = [s[n] for n in names]
        block = es.enter_context(nc.Block())

        tok = lambda t, b: t[b].rearrange("(t p) d -> p t d", p=P)
        head_w = {}
        for n, w, dst in (("q", Wq, wqX), ("k", Wk, wkX), ("v", Wv, wvX)):
            for half in range(2):
                head_w[n, half] = (w[half * H // 2:(half + 1) * H // 2].rearrange("h (c p) e -> p c h e", p=P),
                                   dst[:, :, :, half * 512:(half + 1) * 512])
        for half in range(2):
            head_w["o", half] = (Wo[half * 512:(half + 1) * 512, :].rearrange("(c p) d -> p c d", p=P),
                                 woX[:, :, half * 4:half * 4 + 4, :])
        raw_order = [("q", 0), ("k", 0), ("v", 0), ("q", 1), ("k", 1), ("v", 1), ("o", 0), ("o", 1)]
        raw_sem = [w_q0, w_k0, w_v0, w_q1, w_k1, w_v1, w_o0, w_o1]
        NRAW = len(raw_order)

        def raw_copy(n):
            c = head_w[raw_order[n]][0].shape[1]
            return raw_head[:, n * 1024:(n + 1) * 1024].rearrange("p (c n) -> p c n", c=c)

        raw_at = [[], [3, 4], [5, 6, 7]] + [[]] * 5

        units = []
        qkv_raw = stage0[:, 0:1536].rearrange("p (j d) -> p j d", j=6)
        out_raw = stage0[:, 1536:2048].rearrange("p (j d) -> p j d", j=2)
        w1_raw = stage1[:, 0:1536].rearrange("p (j d) -> p j d", j=NF)
        w2_raw = stage0[:, 0:1536].rearrange("p (j d) -> p j d", j=NF)
        w3_raw = stage1[:, 0:2 * DFF].rearrange("p (j d) -> p j d", j=2)
        for c in range(NC):
            cs = slice(c * P, (c + 1) * P)
            units.append((4, [(j * P, P, qkv_raw[:, j, cs]) for j in (0, 1)], P, wqkvX[:, :, c, 0:256], g1q[:, c:c + 1]))
            units.append((4, [((j - 2) * P, P, qkv_raw[:, j, cs]) for j in (2, 3)], P, wqkvX[:, :, c, 256:512],
                          g1c[:, c:c + 1]))
            units.append((4, [((j - 4) * P, P, qkv_raw[:, j, cs]) for j in (4, 5)], P, wqkvX[:, :, c, 512:768],
                          g1c[:, c:c + 1]))
            units.append((4, [(j * P, P, out_raw[:, j, cs]) for j in (0, 1)], P, woutX[:, :, c, :], None))
        for q, raw, dst in ((5, w1_raw, w1X), (6, w2_raw, w2X)):
            for c in range(NC):
                cs = slice(c * P, (c + 1) * P)
                units.append((q, [(j * P, P, raw[:, j, cs]) for j in range(4)], P, dst[:, :, c, 0:512],
                              g2c[:, c:c + 1]))
                units.append((q, [(0, P, raw[:, 4, cs]), (P, FR, raw[0:FR, 5, cs])], P, dst[:, :, c, 512:DFF],
                              g2c[:, c:c + 1]))
        for c in range(NF):
            rows = P if c < NF - 1 else FR
            units.append((7, [(j * P, P, w3_raw[:, j, c * P:c * P + rows]) for j in range(2)], rows,
                          w3X[0:rows, :, c, :], half_col[0:rows, 0:1]))
        NU = len(units)
        last_unit = {q: max(i for i, w in enumerate(units) if w[0] == q) for q in (4, 5, 6, 7)}
        raw_sems = {4: w_in4, 5: w_in5, 6: w_in6, 7: w_in7}
        unit_at = [list(range(g * NU // (2 * HP), (g + 1) * NU // (2 * HP))) for g in range(2 * HP)]

        bkV = [bkQ, bkK]

        def center(eng):
            for t in range(NT):
                eng.tensor_scalar(xin[:, t, :], xin[:, t, :], mv[:, t, 0:1], rsn[:, t:t + 1], ALU.subtract, ALU.mult)\
                   .then_inc(z_ok, 1)

        @block.sync
        def _(eng):
            def load(b):
                need(eng, zt_p, 1, b, 0)
                eng.dma_start(xin[:, :, :], tok(x, b)).then_inc(x_in, 16)
                need(eng, ct_p, 1, b, 0)
                eng.dma_start(cin[:, :, :], tok(ctx_in, b)).then_inc(c_in, 16)

            def store(b):
                eng.wait_ge(fot, b + 1)
                eng.dma_start(tok(out, b), ot).then_inc(out_d, 16)

            def load_residual(b):
                need(eng, ft1, 2, b, 0)
                eng.dma_start(x1[:, :, :], tok(x, b)).then_inc(xr_in, 16)

            load(0)
            def load_raw(n):
                src, dst = head_w[raw_order[n]][0], raw_copy(n)
                if len(src.shape) == 4:
                    for c in range(NC):
                        eng.dma_start(dst[:, c].rearrange("p (h e) -> p h e", e=HD), src[:, c]).then_inc(raw_sem[n], 16)
                else:
                    for c in range(0, HP // 2, 2):
                        eng.dma_start(dst[:, c:c + 2], src[:, c:c + 2]).then_inc(raw_sem[n], 16)

            def load_rows(dst, w, loaded):
                eng.dma_start(dst[:, 0:NF - 1, :], w[0:(NF - 1) * P, :].rearrange("(j p) d -> p j d", p=P)).then_inc(loaded, 16)
                eng.dma_start(dst[0:FR, NF - 1, :], w[(NF - 1) * P:DFF, :]).then_inc(loaded, 16)

            for n in range(3):
                load_raw(n)
            eng.dma_start(gcol[:, 0:1], g_xattn.partition_broadcast(P)).then_inc(gld, 16)
            eng.dma_start(gcol[:, 1:2], g_ffn.partition_broadcast(P)).then_inc(gld, 16)
            eng.dma_start(wrow[:, :], w_router.partition_broadcast(P)).then_inc(gld, 16)
            eng.dma_start(g1c[:, :], g1.rearrange("(c p) -> p c", p=P), allow_slow_non_contiguous=True).then_inc(rld, 16)
            eng.dma_start(g2c[:, :], g2.rearrange("(c p) -> p c", p=P), allow_slow_non_contiguous=True).then_inc(rld, 16)
            eng.dma_start(qkv_raw, W_qkv.rearrange("(j p) d -> p j d", p=P)).then_inc(w_in4, 16)
            eng.dma_start(out_raw, W_out.rearrange("(j p) d -> p j d", p=P)).then_inc(w_in4, 16)
            for n in range(3, NRAW):
                load_raw(n)
            load_residual(0)
            load_rows(w1_raw, W1, w_in5)
            eng.wait_ge(up, last_unit[4] + 1)
            load_rows(w2_raw, W2, w_in6)
            eng.wait_ge(up, last_unit[5] + 1)
            eng.dma_start(w3_raw, W3.rearrange("(j p) d -> p j d", p=P)).then_inc(w_in7, 16)

            def iteration(i):
                load(i + 1)
                store(i - 2)
                load_residual(i)

            load(1)
            load(2)
            load_residual(1)
            with eng.Fori(2, B - 1) as i:
                iteration(i)
            store(B - 3)
            load_residual(B - 1)
            store(B - 2)
            store(B - 1)
            eng.wait_ge(out_d, 16 * B)

        @block.gpsimd
        def _(eng):
            eng.memset(ident[:, :], 0.0).then_inc(zb, 1)
            eng.memset(mask[:, :], 0.0).then_inc(zb, 1)
            eng.memset(tri[:, :, :], 1.0).then_inc(zb, 1)
            eng.memset(f32(kX[:, :, :, :]), 0.0).then_inc(id1, 1)
            eng.wait_ge(zb, 3)
            eng.affine_select(out=ident[:, :], in_=ident[:, :], compare_op=ALU.not_equal, fill=1.0, base=0,
                              pattern=[[-1, P]], channel_multiplier=1).then_inc(id1, 1)
            eng.affine_select(out=mask[:, P:2 * P], in_=mask[:, P:2 * P], compare_op=ALU.is_ge, fill=BIG, base=0,
                              pattern=[[-1, P]], channel_multiplier=1).then_inc(mk1, 1)
            for t in range(NT):
                eng.affine_select(out=tri[:, t, :], in_=tri[:, t, :], compare_op=ALU.is_gt, fill=0.0, base=t * P,
                                  pattern=[[-1, S]], channel_multiplier=1).then_inc(tri1, 1)
            eng.iota(iota[:, :], pattern=[[1, P]], base=0, channel_multiplier=0,
                     allow_small_or_imprecise_dtypes=True).then_inc(cst, 1)
            eng.memset(mhalf[:, :], -0.5).then_inc(cst, 1)
            eng.memset(half_col[:, :], 0.5).then_inc(cst, 1)
            eng.wait_ge(cst, 3)

            def prep(b):
                eng.wait_ge(st3, b + 1)
                eng.tensor_tensor(rs[:, :], ve[:, :], mhalf[:, :], ALU.pow).then_inc(zr1, 1)
                need_apart(eng, zr1, 1, b, 1, pool_passed)
                eng.tensor_scalar(rsn[:, :], rs[:, :], -0.125, 1.0, ALU.mult, ALU.mult).then_inc(zr2, 1)

            def prep_z(b):
                need_apart(eng, zr2, 1, b, 1, pool_passed)
                center(eng)

            def y_low(b):
                eng.wait_ge(fyh, b + 1)
                eng.tensor_tensor(yX[:, 1, :, :], y, f32(yX[:, 0, :, :]), ALU.subtract).then_inc(fyl, 1)

            def keep_y(b):
                need(eng, out_d, 16, b, 0)
                need_apart(eng, frs2, 1, b, 1, pool_passed)
                for t in range(NT):
                    eng.tensor_scalar(ot[:, t, :], y[:, t, :], nst[:, t:t + 1], 1.0, ALU.mult, ALU.mult).then_inc(fky, 1)
                eng.wait_ge(fky, b * 2 + 2)
                eng.tensor_tensor(ot, ot, x1[:, :, :], ALU.add).then_inc(ft1, 2)

            def normalise(b, p):
                blk = pm[:, p % 2, :]
                need_apart(eng, rc, 8, b, p + 1, pool_passed)
                for j, o, w in PM_BLOCKS:
                    eng.tensor_scalar(blk[:, o:o + w], blk[:, o:o + w], ri[:, p % 2, j:j + 1], 1.0, ALU.mult,
                                      ALU.mult).then_inc(nm, 1)

            def ln2(b):
                eng.wait_ge(fs3, b + 1)
                eng.tensor_tensor(rs2[:, :], ve2[:, :], mhalf[:, :], ALU.pow).then_inc(fr2, 1)

            def rms1(b):
                eng.wait_ge(fms, b + 1)
                eng.tensor_tensor(rr[:, 0:1], ms[:, 0:1], mhalf[:, 0:1], ALU.pow).then_inc(fr3, 1)

            def rms2(b):
                eng.wait_ge(fm2, b + 1)
                eng.tensor_tensor(rr[:, 1:2], ms[:, 1:2], mhalf[:, 0:1], ALU.pow).then_inc(fr4, 1)

            def iteration(i, attn, main, ahead):
                for p in range(HP):
                    if attn:
                        normalise(i, p)
                    if p == 2 and main:
                        y_low(i - 1)
                    if p == 3 and main:
                        rms1(i - 1)
                        keep_y(i - 1)
                    if p == 1 and main:
                        ln2(i - 1)
                    if p == 5 and ahead:
                        prep(i + 1)
                        prep_z(i + 1)
                    if p == 7 and main:
                        rms2(i - 1)

            prep(0)
            iteration(0, True, False, True)
            iteration(1, True, True, True)
            with eng.Fori(2, B - 1) as i:
                iteration(i, True, True, True)
            iteration(B - 1, True, True, False)
            iteration(B, False, True, False)

        @block.tensor
        def _(eng):
            def product(dst, terms, start=True, stop=True):
                n = len(terms) * 3
                k = 0
                for lhs, rhs in terms:
                    for a, c in ((0, 0), (0, 1), (1, 0)):
                        mm = eng.matmul(dst, lhs(a), rhs(c), start=(start and k == 0), stop=(stop and k == n - 1))
                        k += 1
                return mm

            def prep_T(b):
                eng.wait_ge(z_ok, b * 2 + 2)
                need(eng, q_lo, 8, b, 0)
                for c in range(NC):
                    for t in range(NT):
                        mm = eng.transpose(bkQ[:, c * S + t * P:c * S + t * P + P], xin[:, t, c * P:(c + 1) * P], ident[:, :])
                mm.then_inc(zt_p, 1)
                eng.wait_ge(c_in, b * 16 + 16)
                need(eng, k_lo, 16, b, 0)
                for c in range(NC):
                    for t in range(NT):
                        mm = eng.transpose(bkK[:, c * S + t * P:c * S + t * P + P], cin[:, t, c * P:(c + 1) * P], ident[:, :])
                mm.then_inc(ct_p, 1)

            def proj(b, p):
                cols = slice(p * P, (p + 1) * P)
                if p == 0:
                    eng.wait_ge(z_lo, b + 1)
                elif p in (2, 5):
                    eng.wait_ge(v_lo, b * 4 + p - p // 2)
                else:
                    need(eng, q_lo, 8, b, p)
                product(bkQ[:, 0:S], [(lambda a, c=c: wqX[:, a, c, cols], lambda a, c=c: zX[:, a, c, :]) for c in range(NC)])\
                    .then_inc(qp, 1)
                if p == 0:
                    eng.wait_ge(c_lo, b + 1)
                elif p in (3, 6):
                    eng.wait_ge(v_lo, b * 4 + 2 * (p // 3))
                else:
                    need(eng, k_lo, 16, b, 2 * p)
                product(bkK[:, 0:S], [(lambda a, c=c: wkX[:, a, c, cols], lambda a, c=c: cX[:, a, c, :]) for c in range(NC)])\
                    .then_inc(kp, 1)

            def v_proj(b, half, t):
                p = [sl for sl in V_SLOT if (half, t) in V_SLOT[sl]][0] + 1
                if t == 0:
                    eng.wait_ge(q_lo, b * 8 + p + 1)
                else:
                    eng.wait_ge(k_lo, b * 16 + 2 * p + 2)
                product(bkV[t][:, :], [(lambda a, c=c: cX[:, a, c, t * P:(t + 1) * P],
                                        lambda a, c=c: wvX[:, a, c, half * 512:half * 512 + 512]) for c in range(NC)])\
                    .then_inc(vp, 1)

            def scores(b, p):
                eng.wait_ge(q_lo, b * 8 + p + 1)
                eng.wait_ge(k_lo, b * 16 + 2 * p + 2)
                need(eng, smk, 32, b, 4 * p)
                if p == 2:
                    need(eng, f_x1, 2, b, 0)
                if p == 6:
                    eng.wait_ge(f_x1, b * 2 + 1)
                for qt, dst in ((1, bkS1[:, :].rearrange("p (h k) -> p h k", h=2)),
                                (0, bkS0[:, 0:256].rearrange("p (h k) -> p h k", h=2))):
                    if qt == 0:
                        need(eng, p_lo, 16, b, 2 * p - 2)
                    product(dst, [(lambda a: qX[:, a, qt * P:(qt + 1) * P], lambda a: kX[:, a, :, 0:(qt + 1) * P])])\
                        .then_inc(sp, 1)

            def p_T(b, p, more=True):
                blk = pm[:, p % 2, :]
                eng.wait_ge(nm, b * 32 + 4 * p + 4)
                for hh in range(2):
                    eng.transpose(bkP[:, hh * S:hh * S + P], blk[:, hh * P:(hh + 1) * P], ident[:, :])
                    mm = eng.transpose(bkP[:, hh * S + P:(hh + 1) * S], blk[:, 256 + hh * S:256 + hh * S + P], ident[:, :])
                mm.then_inc(tp, 1)
                if more:
                    eng.wait_ge(smk, b * 32 + 4 * p + 8)
                for hh in range(2):
                    mm = eng.transpose(bkS0[:, 256 + hh * P:256 + (hh + 1) * P], blk[:, 256 + hh * S + P:256 + (hh + 1) * S],
                                       ident[:, :])
                mm.then_inc(tp, 1)

            def pv(b, p):
                half, cols = p // 4, slice((p % 4) * P, (p % 4 + 1) * P)
                eng.wait_ge(p_lo, b * 16 + 2 * p + 2)
                eng.wait_ge(v_lo, b * 4 + 2 * half + 2)
                need(eng, o_lo, 16, b, 2 * p)
                o = bkO[:, :].rearrange("p (h q) -> p h q", h=2)
                product(o, [(lambda a: vX[:, a, half, 0, cols], lambda a: p0X[:, a, :, :])], stop=False)
                product(o[:, :, P:S], [(lambda a: vX[:, a, half, 1, cols], lambda a: p1X[:, a, :, :])], start=False)\
                    .then_inc(ov, 1)

            def wo(b, half, attn=True):
                eng.wait_ge(o_lo, b * 16 + 8 * half + 8)
                if half == 0:
                    eng.wait_ge(smk, b * 32 + 24)
                elif attn:
                    eng.wait_ge(smk, b * 32 + 32 + 8)
                for t in range(NT):
                    mm = product(bkS1[:, t * D:(t + 1) * D],
                                 [(lambda a, c=c: oX[:, a, c, t * P:(t + 1) * P], lambda a, c=c: woX[:, a, half * 4 + c, :])
                                  for c in range(HP // 2)])
                mm.then_inc(wp, 1)

            def weight_unit(k):
                q, parts, rows, dst, scale = units[k]
                eng.wait_ge(raw_sems[q], 16 if q == 7 else 32)
                if k >= 2:
                    eng.wait_ge(ul, k - 1)
                bank = (bkA, bkB)[k % 2]
                for col, n, src in parts:
                    mm = eng.transpose(bank[0:rows, col:col + n], src, ident[0:n, 0:n])
                mm.then_inc(up, 1)

            def F1(b):
                eng.wait_ge(fsc, b * 2 + 2)
                need(eng, fot, 1, b, 0)
                for t in range(NT):
                    mm = eng.transpose(bkB[:, t * P:(t + 1) * P], sc[:, t:t + 1].to_broadcast([P, P]), ident[:, :])
                mm.then_inc(fp1, 1)

            def F2(b):
                eng.wait_ge(fpm, b * 2 + 2)
                eng.wait_ge(fyl, b + 1)
                k = 0
                for t in range(NT):
                    for a in range(2):
                        mm = eng.matmul(bkA[:, 0:D], perm[:, t, :], yX[:, a, t, :], start=(k == 0), stop=(k == 3))
                        k += 1
                mm.then_inc(fg, 1)
                for t in range(NT):
                    mm = eng.transpose(bkB[:, t * P:(t + 1) * P], f32(perm[:, t, :]), ident[:, :])
                mm.then_inc(fpt, 1)

            def F3(b):
                eng.wait_ge(fh, b + 1)
                eng.wait_ge(fptc, b + 1)
                for c in range(NC):
                    mm = eng.transpose(bkB[:, c * P:(c + 1) * P], h[:, c * P:(c + 1) * P], ident[:, :])
                mm.then_inc(fp3, 1)

            def F4(b):
                eng.wait_ge(fh_lo, b + 1)
                product(bkA[:, :], [(lambda a, c=c: hX[:, a, c, :], lambda a, c=c: wqkvX[:, a, c, 0:512]) for c in range(NC)])\
                    .then_inc(fqk, 1)
                product(bkB[:, 0:D], [(lambda a, c=c: hX[:, a, c, :], lambda a, c=c: wqkvX[:, a, c, 512:768])
                                      for c in range(NC)]).then_inc(fv, 1)

            def F5(b, arrays):
                eng.wait_ge(fq_lo, b * 3 + 3)
                eng.wait_ge(fv_hi, b + 1)
                for a in arrays:
                    bank = (bkA, bkB, bkB)[a]
                    if a == 2:
                        eng.wait_ge(fT, b * 3 + 2)
                    for t in range(4):
                        mm = eng.transpose(bank[:, t * P:(t + 1) * P],
                                           f32(qkp[:, a, 4 * t:4 * t + 4, :]).rearrange("p h e -> p (h e)"), ident[:, :])
                    mm.then_inc(f5p, 1)

            def F6(b, r):
                eng.wait_ge(fT, b * 3 + 3)
                if r >= 2:
                    need(eng, fpf, 4, b, r - 1)
                bank = (bkB, bkA)[r % 2]
                rows = slice(32 * r, 32 * r + 32)
                for t in range(4):
                    for a in (1, 2):
                        mm = eng.matmul(bank[:, t * P:(t + 1) * P], qkT[rows, 0, t, :], qkT[rows, a, t, :],
                                        start=(a == 1), stop=(a == 2))
                mm.then_inc(fsp, 1)

            def F7(b, r):
                eng.wait_ge(fex, b * 16 + 4 * r + 4)
                if r == 3:
                    eng.wait_ge(fof, b * 2 + 1)
                bank = (bkB, bkA)[r % 2]
                for t in range(4):
                    mm = eng.transpose(bank[:, t * P:(t + 1) * P], sf[:, r % 2, t, :], ident[:, :])
                mm.then_inc(fpp, 1)

            def F8(b, g):
                eng.wait_ge(fpf, b * 4 + 2 * g + 2)
                if g == 0:
                    eng.wait_ge(fsm, b * 16 + 16)
                for r in (2 * g, 2 * g + 1):
                    for t in range(4):
                        hd = 4 * t + r
                        mm = eng.matmul(bkA[:, hd * FHD:(hd + 1) * FHD], pf[:, r % 2, t, :], vf[:, hd * FHD:(hd + 1) * FHD],
                                        start=True, stop=True)
                mm.then_inc(fpo, 1)

            def F9(b):
                eng.wait_ge(fof, b * 2 + 2)
                for c in range(NC):
                    mm = eng.transpose(bkB[:, c * P:(c + 1) * P], oh[:, c * P:(c + 1) * P], ident[:, :])
                mm.then_inc(fp9, 1)

            def F10(b):
                eng.wait_ge(fo_lo, b + 1)
                product(bkA[:, 0:D], [(lambda a, c=c: hX[:, a, c, :], lambda a, c=c: woutX[:, a, c, :]) for c in range(NC)])\
                    .then_inc(fup, 1)

            def F11(b):
                eng.wait_ge(fh2, b + 1)
                for c in range(NC):
                    mm = eng.transpose(bkB[:, c * P:(c + 1) * P], h[:, c * P:(c + 1) * P], ident[:, :])
                mm.then_inc(fp11, 1)

            def F12(b, j):
                o, w = FCH[j]
                if j == 0:
                    eng.wait_ge(fh2_lo, b + 1)
                else:
                    eng.wait_ge(fgl, b * 2 + 1)
                product(bkA[:, 0:w], [(lambda a, c=c: hX[:, a, c, :], lambda a, c=c: w1X[:, a, c, o:o + w]) for c in range(NC)])
                product(bkB[:, 0:w], [(lambda a, c=c: hX[:, a, c, :], lambda a, c=c: w2X[:, a, c, o:o + w]) for c in range(NC)])\
                    .then_inc(f12, 1)

            def F13(b):
                eng.wait_ge(fgl, b * 2 + 2)
                for c in range(4):
                    mm = eng.transpose(bkA[:, c * P:(c + 1) * P], gb[:, c * P:(c + 1) * P], ident[:, :])
                mm.then_inc(f13, 1)
                eng.transpose(bkB[:, 0:P], gb[:, 4 * P:5 * P], ident[:, :])
                eng.transpose(bkB[0:FR, P:2 * P], gb[:, 5 * P:DFF], ident[:, :]).then_inc(f13, 1)

            def F14(b):
                eng.wait_ge(fg_lo, b * 3 + 3)
                rows = lambda c: P if c < NF - 1 else FR
                product(bkA[:, 0:D], [(lambda a, c=c: gX[0:rows(c), a, c, :], lambda a, c=c: w3X[0:rows(c), a, c, :])
                                      for c in range(NF)]).then_inc(fw3, 1)

            def F15(b):
                eng.wait_ge(fx_lo, b + 1)
                for t in range(NT):
                    for a in range(2):
                        mm = eng.matmul(bkB[:, t * D:(t + 1) * D], permT[:, t * P:(t + 1) * P], xpX[:, a, :],
                                        start=(a == 0), stop=(a == 1))
                mm.then_inc(fsca, 1)

            def iteration(i, attn, before, main, tail, ahead, weights=False):
                for p in range(HP):
                    if attn:
                        scores(i, p)
                    if p in W_NEED and weights:
                        eng.wait_ge(wl, W_NEED[p])
                    if p == 6 and main:
                        F7(i - 1, 1)
                    if p < 7 and attn:
                        proj(i, p + 1)
                    if p == 7 and main:
                        F7(i - 1, 3)
                    if weights:
                        for k in unit_at[2 * p]:
                            weight_unit(k)
                    if p == 2 and tail:
                        F15(i - 2)
                    if p == 1 and tail:
                        F12(i - 2, 1)
                    if p == 7 and ahead:
                        prep_T(i + 1)
                    if p < 2 and before:
                        pv(i - 1, HP - 2 + p)
                    if p == 4 and main:
                        F3(i - 1)
                    if p == 5 and main:
                        F5(i - 1, (2,))
                    if p == 6 and main:
                        F6(i - 1, 2)
                    if p == 6 and main:
                        F6(i - 1, 3)
                    if p == 7 and main:
                        F8(i - 1, 1)
                    if p == 0 and tail:
                        F11(i - 2)
                    if p >= 2 and attn:
                        pv(i, p - 2)
                    if p >= 1 and attn:
                        p_T(i, p - 1)
                    if p == 0 and before:
                        p_T(i - 1, HP - 1, more=attn)
                    if p == 1 and tail:
                        F13(i - 2)
                    if p == 3 and main:
                        F2(i - 1)
                    if p == 4 and main:
                        F4(i - 1)
                    if p == 5 and main:
                        F6(i - 1, 0)
                    if p == 5 and main:
                        F6(i - 1, 1)
                    if p == 6 and main:
                        F8(i - 1, 0)
                    if p == 7 and main:
                        F9(i - 1)
                    if p == 5 and attn:
                        wo(i, 0)
                    if p == 1 and before:
                        wo(i - 1, 1, attn)
                    if attn:
                        for half, t in V_SLOT.get(p, ()):
                            v_proj(i, half, t)
                    if p == 7 and ahead:
                        proj(i + 1, 0)
                    if weights:
                        for k in unit_at[2 * p + 1]:
                            weight_unit(k)
                    if p == 1 and tail:
                        F14(i - 2)
                    if p == 0 and tail:
                        F12(i - 2, 0)
                    if p == 2 and main:
                        F1(i - 1)
                    if p == 4 and main:
                        F5(i - 1, (0, 1))
                    if p == 5 and main:
                        F7(i - 1, 0)
                    if p == 6 and main:
                        F7(i - 1, 2)
                    if p == 7 and main:
                        F10(i - 1)

            eng.wait_ge(id1, 2)
            prep_T(0)
            eng.wait_ge(wl, 2)
            proj(0, 0)
            iteration(0, True, False, False, False, True, weights=True)
            eng.wait_ge(ul, NU)
            iteration(1, True, True, True, False, True)
            with eng.Fori(2, B - 1) as i:
                iteration(i, True, True, True, True, True)
            iteration(B - 1, True, True, True, True, False)
            iteration(B, False, True, True, True, False)
            iteration(B + 1, False, False, False, True, False)

        @block.scalar
        def _(eng):
            def high(dst, src, done):
                eng.activation(dst, src, ACT.Copy).then_inc(done, 1)

            def raw_hi(n):
                dst = head_w[raw_order[n]][1]
                eng.wait_ge(raw_sem[n], 32)
                high(dst[:, 0], raw_copy(n), wh)

            def prep_hi(b):
                eng.wait_ge(zt_p, b + 1)
                high(zX[:, 0, :, :], bkQ[:, :].rearrange("p (c s) -> p c s", c=NC), z_hi)
                eng.wait_ge(ct_p, b + 1)
                high(cX[:, 0, :, :], bkK[:, :].rearrange("p (c s) -> p c s", c=NC), c_hi)

            def v_hi_(b, half, t):
                eng.wait_ge(vp, b * 4 + 2 * half + t + 1)
                high(vX[:, 0, half, t, :], bkV[t][:, :], v_hi)

            def qk_hi(b, p):
                eng.wait_ge(qp, b * 8 + p + 1)
                high(qX[:, 0, :], bkQ[:, 0:S], q_hi)
                eng.wait_ge(kp, b * 8 + p + 1)
                for hh in range(2):
                    r = slice(64 * hh, 64 * hh + 64)
                    high(kX[r, 0, hh, :], bkK[r, 0:S], k_hi)

            def exp(b, p):
                blk = pm[:, p % 2, :]
                for k, (j, o, w) in enumerate(PM_BLOCKS):
                    eng.wait_ge(smk, b * 32 + 4 * p + k + 1)
                    eng.activation(blk[:, o:o + w], blk[:, o:o + w], ACT.Exp, bias=mn[:, p % 2, j:j + 1], scale=-1.0,
                                   accum_out=sm[:, p % 2, j:j + 1]).then_inc(ex, 1)

            def p_hi_(b, p):
                eng.wait_ge(tp, b * 16 + 2 * p + 1)
                high(p0X[:, 0, :, :], bkP[:, :].rearrange("p (h q) -> p h q", h=2), p_hi)
                eng.wait_ge(tp, b * 16 + 2 * p + 2)
                high(p1X[:, 0, :, :], bkS0[:, 256:512].rearrange("p (h q) -> p h q", h=2), p_hi)

            def o_hi_(b, p):
                eng.wait_ge(ov, b * 8 + p + 1)
                for hh in range(2):
                    r = slice(64 * hh, 64 * hh + 64)
                    high(oX[r, 0, p % 4, :], bkO[r, hh * S:(hh + 1) * S], o_hi)

            def A0(b):
                eng.wait_ge(fy, b * 2 + 2)
                high(yX[:, 0, :, :], y, fyh)

            def A2(b):
                eng.wait_ge(fg, b + 1)
                eng.activation(xs, bkA[:, 0:D], ACT.Copy).then_inc(fxs, 1)
                eng.wait_ge(fpt, b + 1)
                high(permT[:, :], bkB[:, 0:S], fptc)

            def hX_hi(src_ready, done):
                def go(b):
                    eng.wait_ge(src_ready, b + 1)
                    high(hX[:, 0, :, :], bkB[:, 0:D].rearrange("p (c n) -> p c n", c=NC), done)
                return go

            A3, A9, A11 = hX_hi(fp3, fh_hi), hX_hi(fp9, fo_hi), hX_hi(fp11, fh2_hi)

            def A4(b):
                eng.wait_ge(fqk, b + 1)
                q_ = bkA[:, 0:D].rearrange("p (h e) -> p h e", h=FH)
                k_ = bkA[:, D:2 * D].rearrange("p (h e) -> p h e", h=FH)
                high(qkp[:, 0, :, 0:16], q_, fq_hi)
                high(qkp[:, 1, :, 0:16], k_, fq_hi)
                high(qkp[:, 1, :, 16:32], k_, fq_hi)
                eng.wait_ge(fv, b + 1)
                eng.activation(vf[:, :], bkB[:, 0:D], ACT.Copy).then_inc(fv_hi, 1)

            def A5(b, arrays):
                for a in arrays:
                    bank = (bkA, bkB, bkB)[a]
                    eng.wait_ge(f5p, b * 3 + a + 1)
                    high(qkT[:, a, :, :], bank[:, :].rearrange("p (t n) -> p t n", t=4), fT)

            def A6(b, r):
                for t in range(4):
                    hd = 4 * t + r
                    eng.wait_ge(fsm, b * 16 + 4 * r + t + 1)
                    eng.activation(sf[:, r % 2, t, :], sf[:, r % 2, t, :], ACT.Exp, bias=mf[:, hd:hd + 1], scale=-1.0,
                                   accum_out=sumf[:, hd:hd + 1]).then_inc(fex, 1)

            def A7(b, r):
                eng.wait_ge(fpp, b * 4 + r + 1)
                bank = (bkB, bkA)[r % 2]
                eng.activation(pf[:, r % 2, :, :], bank[:, :].rearrange("p (t n) -> p t n", t=4), ACT.Copy).then_inc(fpf, 1)

            def A12(b, j):
                eng.wait_ge(f12, b * 2 + j + 1)
                w = FCH[j][1]
                eng.activation(eb[:, 0:w], bkA[:, 0:w], ACT.Tanh, scale=0.5).then_inc(fe, 1)

            def A13(b):
                eng.wait_ge(f13, b * 2 + 1)
                high(gX[:, 0, 0:4, :], bkA[:, :].rearrange("p (c n) -> p c n", c=4), fg_hi)
                eng.wait_ge(f13, b * 2 + 2)
                high(gX[:, 0, 4, :], bkB[:, 0:P], fg_hi)
                high(gX[0:FR, 0, 5, :], bkB[0:FR, P:2 * P], fg_hi)

            def A14(b):
                eng.wait_ge(fxp, b + 1)
                high(xpX[:, 0, :], h[:, :], fx_hi)

            def weight_hi(k):
                q, parts, rows, dst, scale = units[k]
                w = dst.shape[-1]
                bank = (bkA, bkB)[k % 2]
                if k == 0:
                    eng.wait_ge(gsc, 1)
                if k == last_unit[4] + 1:
                    eng.wait_ge(wl, NRAW)
                eng.wait_ge(up, k + 1)
                if scale is None:
                    high(dst[:, 0, :], bank[0:rows, 0:w], uh)
                else:
                    eng.activation(dst[:, 0, :], bank[0:rows, 0:w], ACT.Identity, scale=scale).then_inc(uh, 1)

            def iteration(i, attn, before, main, tail, ahead, weights=False):
                for p in range(HP):
                    if p == 6 and main:
                        A7(i - 1, 1)
                    if p < 7 and attn:
                        qk_hi(i, p + 1)
                    if p == 7 and main:
                        A7(i - 1, 3)
                    if weights:
                        for k in unit_at[2 * p]:
                            weight_hi(k)
                    if p == 1 and tail:
                        A12(i - 2, 1)
                    if p == 7 and ahead:
                        prep_hi(i + 1)
                    if p == 4 and main:
                        A3(i - 1)
                    if p == 5 and main:
                        A5(i - 1, (2,))
                    if attn and p not in (1, 3, 5):
                        exp(i, p)
                    if p == 0 and tail:
                        A11(i - 2)
                    if p >= 2 and attn:
                        o_hi_(i, p - 2)
                    if p < 2 and before:
                        o_hi_(i - 1, HP - 2 + p)
                    if p >= 1 and attn:
                        p_hi_(i, p - 1)
                    if p == 0 and before:
                        p_hi_(i - 1, HP - 1)
                    if attn and p in (1, 3, 5):
                        exp(i, p)
                    if p == 1 and tail:
                        A13(i - 2)
                    if p == 6 and main:
                        A6(i - 1, 2)
                    if p == 6 and main:
                        A6(i - 1, 3)
                    if p == 2 and main:
                        A0(i - 1)
                    if p == 4 and main:
                        A4(i - 1)
                    if p == 7 and main:
                        A9(i - 1)
                    if p == 5 and main:
                        A6(i - 1, 0)
                    if p == 5 and main:
                        A6(i - 1, 1)
                    if attn:
                        for half, t in V_SLOT.get(p, ()):
                            v_hi_(i, half, t)
                    if p == 3 and main:
                        A2(i - 1)
                    if p == 7 and ahead:
                        qk_hi(i + 1, 0)
                    if weights:
                        for n in raw_at[p]:
                            raw_hi(n)
                        for k in unit_at[2 * p + 1]:
                            weight_hi(k)
                    if p == 1 and tail:
                        A14(i - 2)
                    if p == 0 and tail:
                        A12(i - 2, 0)
                    if p == 4 and main:
                        A5(i - 1, (0, 1))
                    if p == 5 and main:
                        A7(i - 1, 0)
                    if p == 6 and main:
                        A7(i - 1, 2)

            raw_hi(0)
            prep_hi(0)
            raw_hi(1)
            eng.wait_ge(gld, 48)
            eng.activation(tg[:, :], gcol[:, :], ACT.Tanh).then_inc(th, 1)
            qk_hi(0, 0)
            raw_hi(2)
            iteration(0, True, False, False, False, True, weights=True)
            iteration(1, True, True, True, False, True)
            with eng.Fori(2, B - 1) as i:
                iteration(i, True, True, True, True, True)
            iteration(B - 1, True, True, True, True, False)
            iteration(B, False, True, True, True, False)
            iteration(B + 1, False, False, False, True, False)

        @block.vector
        def _(eng):
            def low(dst, src, hi, done):
                eng.tensor_tensor(dst, src, f32(hi), ALU.subtract).then_inc(done, 1)

            def prep_stats(b):
                eng.wait_ge(x_in, b * 16 + 16)
                for t in range(NT):
                    eng.bn_stats(bst[:, t, :], xin[:, t, :]).then_inc(st1, 1)
                need_apart(eng, st1, 2, b, 2, dve_passed)
                for t in range(NT):
                    eng.bn_aggr(mv[:, t, :], bst[:, t, :]).then_inc(st2, 1)
                eng.wait_ge(st2, b * 2 + 2)
                eng.tensor_scalar(ve[:, :], mv[:, :, 1], 1e-5, None, ALU.add).then_inc(st3, 1)

            def prep_lo(b):
                eng.wait_ge(z_hi, b + 1)
                low(zX[:, 1, :, :], bkQ[:, :].rearrange("p (c s) -> p c s", c=NC), zX[:, 0, :, :], z_lo)
                eng.wait_ge(c_hi, b + 1)
                low(cX[:, 1, :, :], bkK[:, :].rearrange("p (c s) -> p c s", c=NC), cX[:, 0, :, :], c_lo)

            def v_lo_(b, half, t):
                eng.wait_ge(v_hi, b * 4 + 2 * half + t + 1)
                low(vX[:, 1, half, t, :], bkV[t][:, :], vX[:, 0, half, t, :], v_lo)

            def qk_lo(b, p):
                eng.wait_ge(q_hi, b * 8 + p + 1)
                low(qX[:, 1, :], bkQ[:, 0:S], qX[:, 0, :], q_lo)
                eng.wait_ge(k_hi, b * 16 + 2 * p + 2)
                for hh in range(2):
                    r = slice(64 * hh, 64 * hh + 64)
                    low(kX[r, 1, hh, :], bkK[r, 0:S], kX[r, 0, hh, :], k_lo)

            def mask_min(b, p):
                blk = pm[:, p % 2, :]
                for k, (j, o, w) in enumerate(PM_BLOCKS):
                    src = bkS0[:, j * P:(j + 1) * P] if j < 2 else bkS1[:, (j - 2) * S:(j - 1) * S]
                    if k in (0, 2):
                        need_apart(eng, sp, 16, b, 2 * p + k // 2 + 1, dve_passed)
                    eng.tensor_tensor_reduce(blk[:, o:o + w], src, mask[:, 2 * P - w:2 * P], 1.0, 3e38, ALU.add, ALU.min,
                                             mn[:, p % 2, j:j + 1]).then_inc(smk, 1)

            def recip(b, p):
                eng.wait_ge(ex, b * 32 + 4 * p + 4)
                eng.reciprocal(ri[:, p % 2, :], sm[:, p % 2, :]).then_inc(rc, 1)

            def p_lo_(b, p):
                eng.wait_ge(p_hi, b * 16 + 2 * p + 1)
                low(p0X[:, 1, :, :], bkP[:, :].rearrange("p (h q) -> p h q", h=2), p0X[:, 0, :, :], p_lo)
                eng.wait_ge(p_hi, b * 16 + 2 * p + 2)
                low(p1X[:, 1, :, :], bkS0[:, 256:512].rearrange("p (h q) -> p h q", h=2), p1X[:, 0, :, :], p_lo)

            def o_lo_(b, p):
                eng.wait_ge(o_hi, b * 16 + 2 * p + 2)
                for hh in range(2):
                    r = slice(64 * hh, 64 * hh + 64)
                    low(oX[r, 1, p % 4, :], bkO[r, hh * S:(hh + 1) * S], oX[r, 0, p % 4, :], o_lo)

            wo_out = bkS1[:, :].rearrange("p (t d) -> p t d", t=NT)

            def add_wo(b, half):
                eng.wait_ge(wp, b * 2 + half + 1)
                if half == 0:
                    eng.wait_ge(xr_in, b * 16 + 16)
                else:
                    eng.wait_ge(f_x1, b * 2 + 1)
                eng.scalar_tensor_tensor(out=x1[:, :, :], in0=wo_out, scalar=tg[:, 0:1], in1=x1[:, :, :], op0=ALU.mult,
                                         op1=ALU.add).then_inc(f_x1, 1)

            def V0a(b):
                eng.wait_ge(f_x1, b * 2 + 2)
                for t in range(NT):
                    eng.bn_stats(bst2[:, t, :], x1[:, t, :]).then_inc(fs1, 1)
                need_apart(eng, fs1, 2, b, 2, dve_passed)
                for t in range(NT):
                    eng.bn_aggr(mv2[:, t, :], bst2[:, t, :]).then_inc(fs2, 1)
                eng.wait_ge(fs2, b * 2 + 2)
                eng.tensor_scalar(ve2[:, :], mv2[:, :, 1], 1e-5, None, ALU.add).then_inc(fs3, 1)

            def V0b(b):
                eng.wait_ge(fr2, b + 1)
                for t in range(NT):
                    eng.tensor_scalar(y[:, t, :], x1[:, t, :], mv2[:, t, 0:1], rs2[:, t:t + 1], ALU.subtract, ALU.mult)\
                       .then_inc(fy, 1)
                eng.wait_ge(fy, b * 2 + 2)
                for t in range(NT):
                    eng.tensor_tensor_reduce(junk[:, t, :], y[:, t, :], wrow[:, :], 1.0, 0.0, ALU.mult, ALU.add, sc[:, t:t + 1])\
                       .then_inc(fsc, 1)

            def V1(b):
                eng.wait_ge(fp1, b + 1)
                for t in range(NT):
                    eng.tensor_scalar(junk[:, 2 * t, :], bkB[:, 0:S], sc[:, t:t + 1], None, ALU.is_gt, ALU.add,
                                      accum_out=ra[:, t:t + 1]).then_inc(frk, 1)
                    eng.scalar_tensor_tensor(out=junk[:, 2 * t + 1, :], in0=bkB[:, 0:S], scalar=sc[:, t:t + 1], in1=tri[:, t, :],
                                             op0=ALU.is_equal, op1=ALU.mult, accum_out=rb[:, t:t + 1]).then_inc(frk, 1)
                eng.wait_ge(frk, b * 4 + 4)
                eng.tensor_tensor(rank[:, :], ra[:, :], rb[:, :], ALU.add).then_inc(frs, 1)
                eng.wait_ge(frs, b + 1)
                for t in range(NT):
                    eng.tensor_scalar(perm[:, t, :], iota[:, :], rank[:, t:t + 1], None, ALU.is_equal).then_inc(fpm, 1)

            def V2(b):
                eng.tensor_scalar(nst[:, :], rank[:, :], float(CAP), tg[:, 1:2], ALU.is_ge, ALU.mult).then_inc(frs2, 1)
                eng.wait_ge(fxs, b + 1)
                eng.tensor_tensor_reduce(h[:, :], xs, xs, 1.0 / D, 1e-6, ALU.mult, ALU.add, ms[:, 0:1]).then_inc(fms, 1)

            def V2b(b):
                eng.wait_ge(fr3, b + 1)
                eng.tensor_scalar(h[:, :], xs, rr[:, 0:1], None, ALU.mult).then_inc(fh, 1)

            def hX_lo(src_ready, done):
                def go(b):
                    eng.wait_ge(src_ready, b + 1)
                    low(hX[:, 1, :, :], bkB[:, 0:D].rearrange("p (c n) -> p c n", c=NC), hX[:, 0, :, :], done)
                return go

            V3, V9, V11 = hX_lo(fh_hi, fh_lo), hX_lo(fo_hi, fo_lo), hX_lo(fh2_hi, fh2_lo)

            def V4(b):
                eng.wait_ge(fq_hi, b * 3 + 3)
                q_ = bkA[:, 0:D].rearrange("p (h e) -> p h e", h=FH)
                k_ = bkA[:, D:2 * D].rearrange("p (h e) -> p h e", h=FH)
                low(qkp[:, 0, :, 16:32], q_, qkp[:, 0, :, 0:16], fq_lo)
                low(qkp[:, 2, :, 0:16], k_, qkp[:, 1, :, 0:16], fq_lo)
                low(qkp[:, 2, :, 16:32], k_, qkp[:, 1, :, 0:16], fq_lo)

            def V6(b, r):
                need_apart(eng, fsp, 4, b, r + 1, dve_passed)
                bank = (bkB, bkA)[r % 2]
                for t in range(4):
                    hd = 4 * t + r
                    eng.tensor_tensor_reduce(sf[:, r % 2, t, :], bank[:, t * P:(t + 1) * P], mask[:, P:2 * P], 1.0, 3e38,
                                             ALU.add, ALU.min, mf[:, hd:hd + 1]).then_inc(fsm, 1)

            def V8(b, g):
                eng.wait_ge(fex, b * 16 + 8 * g + 8)
                rv = rif[:, :].rearrange("p (t r) -> p t r", r=4)[:, :, 2 * g:2 * g + 2]
                eng.reciprocal(rv, sumf[:, :].rearrange("p (t r) -> p t r", r=4)[:, :, 2 * g:2 * g + 2]).then_inc(frc, 1)
                eng.wait_ge(frc, b * 2 + g + 1)
                eng.wait_ge(fpo, b * 2 + g + 1)
                po = bkA[:, 0:D].rearrange("p (t r e) -> p t r e", t=4, r=4)[:, :, 2 * g:2 * g + 2, :]
                oo = oh[:, :].rearrange("p (t r e) -> p t r e", t=4, r=4)[:, :, 2 * g:2 * g + 2, :]
                eng.tensor_tensor(oo, po, rv.unsqueeze(3).to_broadcast([P, 4, 2, FHD]), ALU.mult).then_inc(fof, 1)

            def V10(b):
                eng.wait_ge(fup, b + 1)
                eng.tensor_tensor(u, bkA[:, 0:D], xs, ALU.add).then_inc(fu, 1)
                eng.wait_ge(fu, b + 1)
                eng.tensor_tensor_reduce(h[:, :], u, u, 1.0 / D, 1e-6, ALU.mult, ALU.add, ms[:, 1:2]).then_inc(fm2, 1)
                eng.wait_ge(fr4, b + 1)
                eng.tensor_scalar(h[:, :], u, rr[:, 1:2], None, ALU.mult).then_inc(fh2, 1)

            def V12(b, j):
                o, w = FCH[j]
                eng.wait_ge(fe, b * 2 + j + 1)
                eng.scalar_tensor_tensor(out=eb[:, 0:w], in0=eb[:, 0:w], scalar=1.0, in1=bkA[:, 0:w], op0=ALU.add,
                                         op1=ALU.mult).then_inc(fe3, 1)
                eng.wait_ge(fe3, b * 2 + j + 1)
                eng.tensor_tensor(gb[:, o:o + w], bkB[:, 0:w], eb[:, 0:w], ALU.mult).then_inc(fgl, 1)

            def V13(b):
                eng.wait_ge(fg_hi, b * 3 + 1)
                low(gX[:, 1, 0:4, :], bkA[:, :].rearrange("p (c n) -> p c n", c=4), gX[:, 0, 0:4, :], fg_lo)
                eng.wait_ge(fg_hi, b * 3 + 3)
                low(gX[:, 1, 4, :], bkB[:, 0:P], gX[:, 0, 4, :], fg_lo)
                low(gX[0:FR, 1, 5, :], bkB[0:FR, P:2 * P], gX[0:FR, 0, 5, :], fg_lo)

            def V14(b):
                eng.wait_ge(fw3, b + 1)
                eng.tensor_tensor(h[:, :], bkA[:, 0:D], u, ALU.add).then_inc(fxp, 1)
                eng.wait_ge(fx_hi, b + 1)
                low(xpX[:, 1, :], h[:, :], xpX[:, 0, :], fx_lo)

            def V15(b):
                eng.wait_ge(ft1, b * 2 + 2)
                eng.wait_ge(fsca, b + 1)
                eng.scalar_tensor_tensor(out=ot, in0=bkB[:, :].rearrange("p (t d) -> p t d", t=NT), scalar=tg[:, 1:2], in1=ot,
                                         op0=ALU.mult, op1=ALU.add).then_inc(fot, 1)

            def weight_lo(k):
                q, parts, rows, dst, scale = units[k]
                w = dst.shape[-1]
                bank = (bkA, bkB)[k % 2]
                eng.wait_ge(uh, k + 1)
                if scale is None:
                    low(dst[:, 1, :], bank[0:rows, 0:w], dst[:, 0, :], ul)
                else:
                    eng.scalar_tensor_tensor(out=dst[:, 1, :], in0=bank[0:rows, 0:w], scalar=scale, in1=f32(dst[:, 0, :]),
                                             op0=ALU.mult, op1=ALU.subtract).then_inc(ul, 1)

            def raw_lo(n):
                dst = head_w[raw_order[n]][1]
                eng.wait_ge(wh, n + 1)
                low(dst[:, 1], raw_copy(n), dst[:, 0], wl)

            def iteration(i, attn, before, main, tail, ahead, weights=False):
                for p in range(HP):
                    if attn:
                        mask_min(i, p)
                    if p == 2 and main:
                        V0b(i - 1)
                    if p < 7 and attn:
                        qk_lo(i, p + 1)
                    if weights:
                        for k in unit_at[2 * p]:
                            weight_lo(k)
                    if p == 2 and tail:
                        V15(i - 2)
                    if p == 1 and tail:
                        V12(i - 2, 1)
                    if p == 7 and ahead:
                        prep_lo(i + 1)
                    if p == 4 and main:
                        V3(i - 1)
                    if p == 6 and main:
                        V6(i - 1, 2)
                    if p == 6 and main:
                        V6(i - 1, 3)
                    if p == 7 and main:
                        V8(i - 1, 1)
                    if p >= 2 and attn:
                        o_lo_(i, p - 2)
                    if p == 0 and tail:
                        V11(i - 2)
                    if p < 2 and before:
                        o_lo_(i - 1, HP - 2 + p)
                    if p >= 1 and attn:
                        p_lo_(i, p - 1)
                    if p == 0 and before:
                        p_lo_(i - 1, HP - 1)
                    if attn:
                        recip(i, p)
                    if p == 1 and tail:
                        V13(i - 2)
                    if p == 4 and main:
                        V4(i - 1)
                    if p == 5 and main:
                        V6(i - 1, 0)
                    if p == 5 and main:
                        V6(i - 1, 1)
                    if p == 6 and main:
                        V8(i - 1, 0)
                    if p == 7 and main:
                        V9(i - 1)
                    if p == 5 and attn:
                        add_wo(i, 0)
                    if p == 1 and before:
                        add_wo(i - 1, 1)
                    if p == 1 and before:
                        V0a(i - 1)
                    if attn:
                        for half, t in V_SLOT.get(p, ()):
                            v_lo_(i, half, t)
                    if p == 3 and main:
                        V2(i - 1)
                    if p == 7 and ahead:
                        qk_lo(i + 1, 0)
                    if weights:
                        for n in raw_at[p]:
                            raw_lo(n)
                        for k in unit_at[2 * p + 1]:
                            weight_lo(k)
                    if p == 1 and tail:
                        V14(i - 2)
                    if p == 0 and tail:
                        V12(i - 2, 0)
                    if p == 2 and main:
                        V1(i - 1)
                    if p == 3 and main:
                        V2b(i - 1)
                    if p == 5 and ahead:
                        prep_stats(i + 1)
                    if p == 7 and main:
                        V10(i - 1)

            eng.wait_ge(mk1, 1)
            eng.wait_ge(tri1, NT)
            eng.wait_ge(cst, 3)
            prep_stats(0)
            eng.wait_ge(zr2, 1)
            center(eng)
            raw_lo(0)
            prep_lo(0)
            raw_lo(1)
            qk_lo(0, 0)
            raw_lo(2)
            eng.wait_ge(gld, 48)
            eng.wait_ge(rld, 32)
            eng.wait_ge(th, 1)
            eng.tensor_scalar(g1q[:, :], g1c[:, :], -0.25, 1.0, ALU.mult, ALU.mult).then_inc(gsc, 1)
            iteration(0, True, False, False, False, True, weights=True)
            iteration(1, True, True, True, False, True)
            with eng.Fori(2, B - 1) as i:
                iteration(i, True, True, True, True, True)
            iteration(B - 1, True, True, True, True, False)
            iteration(B, False, True, True, True, False)
            iteration(B + 1, False, False, False, True, False)


_INS = ["x", "ctx_1024", "g_xattn", "g_ffn", "L0_xattn_Wq", "L0_xattn_Wk", "L0_xattn_Wv", "L0_xattn_Wo",
        "L0_ffn_w_router", "L0_ffn_W_qkv", "L0_ffn_W_out", "L0_ffn_g1", "L0_ffn_g2", "L0_ffn_W1", "L0_ffn_W2", "L0_ffn_W3"]


def kernel(**inputs):
    import numpy as np
    import concourse.bacc as bacc
    from concourse import mybir as mb
    from concourse.bass_utils import run_bass_kernel_spmd as run

    nc = bacc.Bacc("TRN2", target_bir_lowering=False, num_devices=1)
    arrays, args = {}, []
    for name in _INS:
        a = np.ascontiguousarray(inputs[name])
        arrays[f"in_{name}"] = a
        args.append(nc.dram_tensor(f"in_{name}", a.shape, mb.dt.from_np(a.dtype), kind="ExternalInput").ap())
    out = nc.dram_tensor("out_0", (B, S, D), mb.dt.float32, kind="ExternalOutput").ap()
    build(nc, *args, out)
    return run(nc, [arrays], core_ids=[0]).results[0]["out_0"]
```
